# Optimizing a Trainium2 kernel written in Bass

```python
import numpy as np
import jax
import jax.numpy as jnp

def _softmax(x, axis=-1):
    return jax.nn.softmax(x, axis=axis)

def _gelu(x):
    return jax.nn.gelu(x, approximate=True)

def _silu(x):
    return jax.nn.silu(x)

def _sigmoid(x):
    return jax.nn.sigmoid(x)

def _layernorm(x, axis=-1, eps=1e-05):
    m = jnp.mean(x, axis=axis, keepdims=True)
    v = jnp.var(x, axis=axis, keepdims=True)
    return (x - m) / jnp.sqrt(v + eps)

def _scatter_add(tgt, idx, src, axis=0):
    return tgt.at[idx].add(src)

def _segment_sum(src, seg, n):
    return jax.ops.segment_sum(src, seg, n)
kernel_name = 'mk_flamingo_gated_d4_seqx_r8_c46f9c'

def setup_inputs(seed: int=0):
    np.random.seed(seed)
    _w = jnp.asarray

    def _rec_inputs():
        import jax
        import jax.numpy as jnp
        _rk = jax.random.key(seed)
        x = -0.0002928 + 1 * jax.random.normal(jax.random.fold_in(_rk, 1), (8, 256, 128), jnp.float32)
        _lenS = 256 - jax.random.randint(jax.random.fold_in(_rk, 7), (8,), 0, max(1, 256 // 4) + 1, jnp.int32)
        _lenS2 = 256 - jax.random.randint(jax.random.fold_in(_rk, 8), (8,), 0, max(1, 256 // 4) + 1, jnp.int32)
        _ctx_1024P = jax.random.normal(jax.random.fold_in(_rk, 11), (8, 16, 128), jnp.float32)
        _ctx_1024c = jax.random.dirichlet(jax.random.fold_in(_rk, 511), 0.3 * jnp.ones((16,), jnp.float32), (8, 256))
        _ctx_1024t = jnp.einsum('bsk,bkd->bsd', _ctx_1024c, _ctx_1024P)
        _ctx_1024t = _ctx_1024t * jax.lax.rsqrt(jnp.mean(jnp.square(_ctx_1024t)) + 1e-12) * 0.953939
        ctx_1024 = -1.39393e-06 + 0.999914 * (_ctx_1024t + 0.3 * jax.random.normal(jax.random.fold_in(_rk, 611), (8, 256, 128), jnp.float32))
        _validS = jnp.arange(256)[None, :] < _lenS[:, None]
        _validS2 = jnp.arange(256)[None, :] < _lenS2[:, None]
        _causal = jnp.tril(jnp.ones((256, 256), dtype=bool))
        mask_BxS2_ik0 = jnp.where(jnp.broadcast_to(_validS2[:, :], (8, 256)), 0, 1).astype(jnp.int32)
        _g = jax.random.normal(jax.random.fold_in(_rk, 9001), (2, 4), jnp.float32)
        _g = jnp.sign(_g) * jnp.maximum(jnp.abs(_g), 1.0) + (_g == 0) * 1.0
        g_xattn = _g[0]
        g_ffn = _g[1]
        return (x, ctx_1024, mask_BxS2_ik0, g_xattn, g_ffn)
    x, ctx_1024, mask_BxS2_ik0, g_xattn, g_ffn = _rec_inputs()

    def _L0_xattn_setup():
        import jax, jax.numpy as jnp
        import numpy as np
        D_MODEL = 128
        NHEAD = 16
        D_K = D_MODEL // NHEAD
        B, S = (2, 256)
        NEG_INF = float('-inf')

        def _split_heads(x):
            b, s, _ = x.shape
            return x.reshape(b, s, NHEAD, D_K).transpose(0, 2, 1, 3)
        key = jax.random.key(seed)
        ks = jax.random.split(key, 12)
        sc = 1.0 / np.sqrt(D_MODEL)
        return {'q': jax.random.normal(ks[0], (B, S, D_MODEL), dtype=jnp.float32), 'k': jax.random.normal(ks[1], (B, S, D_MODEL), dtype=jnp.float32), 'q_mask': jax.random.randint(ks[2], (B, S), 0, 2, dtype=jnp.int32), 'k_mask': jax.random.randint(ks[3], (B, S), 0, 2, dtype=jnp.int32), 'Wq': jax.random.normal(ks[4], (D_MODEL, D_MODEL), dtype=jnp.float32) * sc, 'bq': jnp.zeros((D_MODEL,), dtype=jnp.float32), 'Wk': jax.random.normal(ks[5], (D_MODEL, D_MODEL), dtype=jnp.float32) * sc, 'bk': jnp.zeros((D_MODEL,), dtype=jnp.float32), 'Wv': jax.random.normal(ks[6], (D_MODEL, D_MODEL), dtype=jnp.float32) * sc, 'bv': jnp.zeros((D_MODEL,), dtype=jnp.float32), 'Wo': jax.random.normal(ks[7], (D_MODEL, D_MODEL), dtype=jnp.float32) * sc, 'bo': jnp.zeros((D_MODEL,), dtype=jnp.float32), 'causal_attention': 1}
    _L0_xattn_all = _L0_xattn_setup()
    _L0_xattn_in = {k: v for k, v in _L0_xattn_all.items() if k in ('Wq', 'bq', 'Wk', 'bk', 'Wv', 'bv', 'Wo', 'bo')}
    del _L0_xattn_all

    def _L0_ffn_setup():
        import jax, jax.numpy as jnp
        import numpy as np
        B, S, D, O, E, R, TOP_K = (4, 128, 128, 128, 8, 16, 2)
        SCALING = 32.0 / 16.0
        NEG_INF = -1000000000.0
        key = jax.random.key(seed)
        ks = jax.random.split(key, 6)
        return {'x': jax.random.normal(ks[0], (B, S, D), jnp.float32), 'base_w': jax.random.normal(ks[1], (O, D), jnp.float32) * 0.02, 'base_b': jnp.zeros((O,), jnp.float32), 'lora_A': jax.random.normal(ks[2], (E, D, R), jnp.float32) * 0.02, 'lora_B': jax.random.normal(ks[3], (E, R, O), jnp.float32) * 0.02, 'router_w': jax.random.normal(ks[4], (E, D), jnp.float32) * 0.02, 'router_b': jnp.zeros((E,), jnp.float32)}
    _L0_ffn_all = _L0_ffn_setup()
    _L0_ffn_in = {k: v for k, v in _L0_ffn_all.items() if k in ('base_w', 'base_b', 'lora_A', 'lora_B', 'router_w', 'router_b')}
    del _L0_ffn_all

    def _L1_xattn_setup():
        import jax, jax.numpy as jnp
        import numpy as np
        EMBED_PHI = 128
        EMBED_F = 128
        HIDDEN_F = 128
        N_HEADS = 16
        B, S = (2, 256)
        key = jax.random.key(seed)
        ks = jax.random.split(key, 9)
        sphi = 1.0 / np.sqrt(EMBED_PHI)
        sf = 1.0 / np.sqrt(EMBED_F)
        sh = 1.0 / np.sqrt(HIDDEN_F)
        return {'q': jax.random.normal(ks[0], (B, S, EMBED_PHI), jnp.float32), 'k': jax.random.normal(ks[1], (B, S, EMBED_PHI), jnp.float32), 'v': jax.random.normal(ks[2], (B, S, EMBED_F), jnp.float32), 'Wq': jax.random.normal(ks[3], (HIDDEN_F, EMBED_PHI), jnp.float32) * sphi, 'Wk': jax.random.normal(ks[4], (HIDDEN_F, EMBED_PHI), jnp.float32) * sphi, 'Wv': jax.random.normal(ks[5], (HIDDEN_F, EMBED_F), jnp.float32) * sf, 'bv': jax.random.normal(ks[6], (HIDDEN_F,), jnp.float32) * sf, 'Wo': jax.random.normal(ks[7], (EMBED_F, HIDDEN_F), jnp.float32) * sh, 'bo': jax.random.normal(ks[8], (EMBED_F,), jnp.float32) * sh}
    _L1_xattn_all = _L1_xattn_setup()
    _L1_xattn_in = {k: v for k, v in _L1_xattn_all.items() if k in ('Wq', 'Wk', 'Wv', 'bv', 'Wo', 'bo')}
    del _L1_xattn_all

    def _L1_ffn_setup():
        import jax, jax.numpy as jnp
        import numpy as np
        H = 128
        I = 64
        E = 64
        G = 8
        TOPK_GROUP = 4
        K = 8
        I_SH = 128
        SCALE = 2.5

        def _route(x, router_w, e_bias):
            T = x.shape[0]
            scores = jax.nn.sigmoid(x.astype(jnp.float32) @ router_w.T.astype(jnp.float32))
            sfc = jax.lax.stop_gradient(scores) + e_bias[None, :]
            group_scores = jax.lax.top_k(sfc.reshape(T, G, E // G), 2)[0].sum(-1)
            _, gidx = jax.lax.top_k(group_scores, TOPK_GROUP)
            gmask = jax.nn.one_hot(gidx, G, dtype=sfc.dtype).sum(1)
            smask = jnp.repeat(gmask, E // G, axis=1)
            masked = jnp.where(smask > 0, sfc, 0.0)
            _, topk_idx = jax.lax.top_k(masked, K)
            w = jnp.take_along_axis(scores, topk_idx, axis=1)
            w = w / (w.sum(-1, keepdims=True) + 1e-20)
            return (topk_idx, w * SCALE)
        key = jax.random.key(seed)
        ks = jax.random.split(key, 9)
        s = 0.02
        return {'hidden_states': jax.random.normal(ks[0], (2, 128, H), jnp.float32), 'router_w': jax.random.normal(ks[1], (E, H), jnp.float32) * s, 'e_bias': jnp.zeros((E,), jnp.float32), 'Wg': jax.random.normal(ks[2], (E, H, I), jnp.float32) * s, 'Wu': jax.random.normal(ks[3], (E, H, I), jnp.float32) * s, 'Wd': jax.random.normal(ks[4], (E, I, H), jnp.float32) * s, 'SWg': jax.random.normal(ks[5], (H, I_SH), jnp.float32) * s, 'SWu': jax.random.normal(ks[6], (H, I_SH), jnp.float32) * s, 'SWd': jax.random.normal(ks[7], (I_SH, H), jnp.float32) * s}
    _L1_ffn_all = _L1_ffn_setup()
    _L1_ffn_in = {k: v for k, v in _L1_ffn_all.items() if k in ('router_w', 'e_bias', 'Wg', 'Wu', 'Wd', 'SWg', 'SWu', 'SWd')}
    del _L1_ffn_all

    def _L2_xattn_setup():
        import jax, jax.numpy as jnp
        import numpy as np
        import math
        B, S, D, H = (2, 256, 128, 16)
        DK = D // H

        def _split_heads(x):
            b, s, _ = x.shape
            return x.reshape(b, s, H, DK).transpose(0, 2, 1, 3)
        key = jax.random.key(seed)
        ks = jax.random.split(key, 8)
        q = jax.random.normal(ks[0], (B, S, D), dtype=jnp.float32)
        k = jax.random.normal(ks[1], (B, S, D), dtype=jnp.float32)
        v = jax.random.normal(ks[2], (B, S, D), dtype=jnp.float32)
        mask = jax.random.randint(ks[3], (B, S), 0, 2, dtype=jnp.int32)
        scale = 1.0 / math.sqrt(D)
        w_q = jax.random.normal(ks[4], (D, D), dtype=jnp.float32) * scale
        w_k = jax.random.normal(ks[5], (D, D), dtype=jnp.float32) * scale
        w_v = jax.random.normal(ks[6], (D, D), dtype=jnp.float32) * scale
        w_o = jax.random.normal(ks[7], (D, D), dtype=jnp.float32) * scale
        return {'q': q, 'k': k, 'v': v, 'mask': mask, 'w_q': w_q, 'w_k': w_k, 'w_v': w_v, 'w_o': w_o}
    _L2_xattn_all = _L2_xattn_setup()
    _L2_xattn_in = {k: v for k, v in _L2_xattn_all.items() if k in ('w_q', 'w_k', 'w_v', 'w_o')}
    del _L2_xattn_all

    def _L2_ffn_setup():
        import jax, jax.numpy as jnp
        import numpy as np
        B, S, D, E, F = (2, 256, 128, 14, 256)
        key = jax.random.key(seed)
        k = jax.random.split(key, 4)
        h = jax.random.normal(k[0], (B, S, D), dtype=jnp.float32)
        router_w = jax.random.normal(k[1], (D, E), dtype=jnp.float32) * 0.02
        w1 = jax.random.uniform(k[2], (E, D, F), dtype=jnp.float32, minval=-1.0, maxval=1.0) * float(np.sqrt(6.0 / D))
        w2 = jax.random.uniform(k[3], (E, F, D), dtype=jnp.float32, minval=-1.0, maxval=1.0) * float(np.sqrt(6.0 / F))
        b1 = jnp.zeros((E, F), dtype=jnp.float32)
        b2 = jnp.zeros((E, D), dtype=jnp.float32)
        return {'h': h, 'router_w': router_w, 'w1': w1, 'b1': b1, 'w2': w2, 'b2': b2}
    _L2_ffn_all = _L2_ffn_setup()
    _L2_ffn_in = {k: v for k, v in _L2_ffn_all.items() if k in ('router_w', 'w1', 'b1', 'w2', 'b2')}
    del _L2_ffn_all

    def _L3_xattn_setup():
        import jax, jax.numpy as jnp
        import numpy as np
        EMBED = 128
        HEADS = 16
        HEAD_DIM = EMBED // HEADS
        key = jax.random.key(seed)
        ks = jax.random.split(key, 11)
        B, S, E = (4, 256, EMBED)
        scale = 1.0 / np.sqrt(E)
        inp = {'Q': jax.random.normal(ks[0], (B, S, E), jnp.float32), 'K': jax.random.normal(ks[1], (B, S, E), jnp.float32), 'V': jax.random.normal(ks[2], (B, S, E), jnp.float32), 'Wq': jax.random.normal(ks[3], (E, E), jnp.float32) * scale, 'Wk': jax.random.normal(ks[4], (E, E), jnp.float32) * scale, 'Wv': jax.random.normal(ks[5], (E, E), jnp.float32) * scale, 'Wo': jax.random.normal(ks[6], (E, E), jnp.float32) * scale, 'bq': jax.random.normal(ks[7], (E,), jnp.float32) * 0.01, 'bk': jax.random.normal(ks[8], (E,), jnp.float32) * 0.01, 'bv': jax.random.normal(ks[9], (E,), jnp.float32) * 0.01, 'bo': jax.random.normal(ks[10], (E,), jnp.float32) * 0.01}
        return inp
    _L3_xattn_all = _L3_xattn_setup()
    _L3_xattn_in = {k: v for k, v in _L3_xattn_all.items() if k in ('Wq', 'Wk', 'Wv', 'Wo', 'bq', 'bk', 'bv', 'bo')}
    del _L3_xattn_all

    def _L3_ffn_setup():
        import jax, jax.numpy as jnp
        import numpy as np
        import math
        D = 128
        H = 16
        E = 8
        TOPK = 2
        LAT = D // 2
        KPH = LAT // H
        HD = D // H

        def _forward(hs, q_w, q_b, k_w, k_b, v_w, v_b, o_w, o_b, router_w, router_b, w1, b1, w2, b2):
            B, S, _ = hs.shape
            Q = (hs @ q_w + q_b).reshape(B, S, H, HD).transpose(0, 2, 1, 3)
            K = (hs @ k_w + k_b).reshape(B, S, H, KPH).transpose(0, 2, 1, 3)
            V = (hs @ v_w + v_b).reshape(B, S, H, KPH).transpose(0, 2, 1, 3)
            scores = jnp.einsum('bhsk,bhtk->bhst', Q[..., :KPH], K) / math.sqrt(KPH)
            attn = jax.nn.softmax(scores, axis=-1)
            ao = jnp.einsum('bhst,bhtv->bhsv', attn, V)
            ao = ao.transpose(0, 2, 1, 3).reshape(B, S, H * KPH)
            ao = jnp.concatenate([ao, jnp.zeros((B, S, D - LAT), ao.dtype)], axis=-1)
            mla_out = ao @ o_w + o_b
            probs = jax.nn.softmax(mla_out @ router_w + router_b, axis=-1)
            topw, topi = jax.lax.top_k(probs, TOPK)
            topw = topw / (topw.sum(-1, keepdims=True) + 1e-08)
            combine = jnp.sum(jax.nn.one_hot(topi, E, dtype=probs.dtype) * topw[..., None], axis=-2)
            h1 = jnp.einsum('bsd,edf->ebsf', mla_out, w1) + b1[:, None, None, :]
            h1 = jax.nn.gelu(h1, approximate=False)
            h2 = jnp.einsum('ebsf,efd->ebsd', h1, w2) + b2[:, None, None, :]
            moe_out = jnp.einsum('bse,ebsd->bsd', combine, h2)
            return hs + 0.3 * moe_out
        key = jax.random.key(seed)
        ks = jax.random.split(key, 16)
        s = 0.02
        inp = {'hidden_states': jax.random.normal(ks[0], (2, 256, D), jnp.float32), 'q_w': jax.random.normal(ks[1], (D, D), jnp.float32) * s, 'q_b': jnp.zeros((D,), jnp.float32), 'k_w': jax.random.normal(ks[2], (D, LAT), jnp.float32) * s, 'k_b': jnp.zeros((LAT,), jnp.float32), 'v_w': jax.random.normal(ks[3], (D, LAT), jnp.float32) * s, 'v_b': jnp.zeros((LAT,), jnp.float32), 'o_w': jax.random.normal(ks[4], (D, D), jnp.float32) * s, 'o_b': jnp.zeros((D,), jnp.float32), 'router_w': jax.random.normal(ks[5], (D, E), jnp.float32) * s, 'router_b': jnp.zeros((E,), jnp.float32), 'w1': jax.random.normal(ks[6], (E, D, 2 * D), jnp.float32) * s, 'b1': jnp.zeros((E, 2 * D), jnp.float32), 'w2': jax.random.normal(ks[7], (E, 2 * D, D), jnp.float32) * s, 'b2': jnp.zeros((E, D), jnp.float32)}
        return inp
    _L3_ffn_all = _L3_ffn_setup()
    _L3_ffn_in = {k: v for k, v in _L3_ffn_all.items() if k in ('q_w', 'q_b', 'k_w', 'k_b', 'v_w', 'v_b', 'o_w', 'o_b', 'router_w', 'router_b', 'w1', 'b1', 'w2', 'b2')}
    del _L3_ffn_all
    return {'x': x, 'ctx_1024': ctx_1024, 'mask_BxS2_ik0': mask_BxS2_ik0, 'g_xattn': g_xattn, 'g_ffn': g_ffn, 'L0_xattn_Wq': _L0_xattn_in['Wq'], 'L0_xattn_bq': _L0_xattn_in['bq'], 'L0_xattn_Wk': _L0_xattn_in['Wk'], 'L0_xattn_bk': _L0_xattn_in['bk'], 'L0_xattn_Wv': _L0_xattn_in['Wv'], 'L0_xattn_bv': _L0_xattn_in['bv'], 'L0_xattn_Wo': _L0_xattn_in['Wo'], 'L0_xattn_bo': _L0_xattn_in['bo'], 'L0_ffn_base_w': _L0_ffn_in['base_w'], 'L0_ffn_base_b': _L0_ffn_in['base_b'], 'L0_ffn_lora_A': _L0_ffn_in['lora_A'], 'L0_ffn_lora_B': _L0_ffn_in['lora_B'], 'L0_ffn_router_w': _L0_ffn_in['router_w'], 'L0_ffn_router_b': _L0_ffn_in['router_b'], 'L1_xattn_Wq': _L1_xattn_in['Wq'], 'L1_xattn_Wk': _L1_xattn_in['Wk'], 'L1_xattn_Wv': _L1_xattn_in['Wv'], 'L1_xattn_bv': _L1_xattn_in['bv'], 'L1_xattn_Wo': _L1_xattn_in['Wo'], 'L1_xattn_bo': _L1_xattn_in['bo'], 'L1_ffn_router_w': _L1_ffn_in['router_w'], 'L1_ffn_e_bias': _L1_ffn_in['e_bias'], 'L1_ffn_Wg': _L1_ffn_in['Wg'], 'L1_ffn_Wu': _L1_ffn_in['Wu'], 'L1_ffn_Wd': _L1_ffn_in['Wd'], 'L1_ffn_SWg': _L1_ffn_in['SWg'], 'L1_ffn_SWu': _L1_ffn_in['SWu'], 'L1_ffn_SWd': _L1_ffn_in['SWd'], 'L2_xattn_w_q': _L2_xattn_in['w_q'], 'L2_xattn_w_k': _L2_xattn_in['w_k'], 'L2_xattn_w_v': _L2_xattn_in['w_v'], 'L2_xattn_w_o': _L2_xattn_in['w_o'], 'L2_ffn_router_w': _L2_ffn_in['router_w'], 'L2_ffn_w1': _L2_ffn_in['w1'], 'L2_ffn_b1': _L2_ffn_in['b1'], 'L2_ffn_w2': _L2_ffn_in['w2'], 'L2_ffn_b2': _L2_ffn_in['b2'], 'L3_xattn_Wq': _L3_xattn_in['Wq'], 'L3_xattn_Wk': _L3_xattn_in['Wk'], 'L3_xattn_Wv': _L3_xattn_in['Wv'], 'L3_xattn_Wo': _L3_xattn_in['Wo'], 'L3_xattn_bq': _L3_xattn_in['bq'], 'L3_xattn_bk': _L3_xattn_in['bk'], 'L3_xattn_bv': _L3_xattn_in['bv'], 'L3_xattn_bo': _L3_xattn_in['bo'], 'L3_ffn_q_w': _L3_ffn_in['q_w'], 'L3_ffn_q_b': _L3_ffn_in['q_b'], 'L3_ffn_k_w': _L3_ffn_in['k_w'], 'L3_ffn_k_b': _L3_ffn_in['k_b'], 'L3_ffn_v_w': _L3_ffn_in['v_w'], 'L3_ffn_v_b': _L3_ffn_in['v_b'], 'L3_ffn_o_w': _L3_ffn_in['o_w'], 'L3_ffn_o_b': _L3_ffn_in['o_b'], 'L3_ffn_router_w': _L3_ffn_in['router_w'], 'L3_ffn_router_b': _L3_ffn_in['router_b'], 'L3_ffn_w1': _L3_ffn_in['w1'], 'L3_ffn_b1': _L3_ffn_in['b1'], 'L3_ffn_w2': _L3_ffn_in['w2'], 'L3_ffn_b2': _L3_ffn_in['b2']}

def reference(x, ctx_1024, mask_BxS2_ik0, g_xattn, g_ffn, L0_xattn_Wq, L0_xattn_bq, L0_xattn_Wk, L0_xattn_bk, L0_xattn_Wv, L0_xattn_bv, L0_xattn_Wo, L0_xattn_bo, L0_ffn_base_w, L0_ffn_base_b, L0_ffn_lora_A, L0_ffn_lora_B, L0_ffn_router_w, L0_ffn_router_b, L1_xattn_Wq, L1_xattn_Wk, L1_xattn_Wv, L1_xattn_bv, L1_xattn_Wo, L1_xattn_bo, L1_ffn_router_w, L1_ffn_e_bias, L1_ffn_Wg, L1_ffn_Wu, L1_ffn_Wd, L1_ffn_SWg, L1_ffn_SWu, L1_ffn_SWd, L2_xattn_w_q, L2_xattn_w_k, L2_xattn_w_v, L2_xattn_w_o, L2_ffn_router_w, L2_ffn_w1, L2_ffn_b1, L2_ffn_w2, L2_ffn_b2, L3_xattn_Wq, L3_xattn_Wk, L3_xattn_Wv, L3_xattn_Wo, L3_xattn_bq, L3_xattn_bk, L3_xattn_bv, L3_xattn_bo, L3_ffn_q_w, L3_ffn_q_b, L3_ffn_k_w, L3_ffn_k_b, L3_ffn_v_w, L3_ffn_v_b, L3_ffn_o_w, L3_ffn_o_b, L3_ffn_router_w, L3_ffn_router_b, L3_ffn_w1, L3_ffn_b1, L3_ffn_w2, L3_ffn_b2):
    import jax
    import jax.numpy as jnp

    def _L0_xattn_ref(q, k, q_mask, k_mask, Wq, bq, Wk, bk, Wv, bv, Wo, bo, causal_attention):
        import jax, jax.numpy as jnp
        import numpy as np
        D_MODEL = 128
        NHEAD = 16
        D_K = D_MODEL // NHEAD
        B, S = (2, 256)
        NEG_INF = float('-inf')

        def _split_heads(x):
            b, s, _ = x.shape
            return x.reshape(b, s, NHEAD, D_K).transpose(0, 2, 1, 3)
        v_in = k
        qh = _split_heads(q @ Wq.T + bq)
        kh = _split_heads(k @ Wk.T + bk)
        vh = _split_heads(v_in @ Wv.T + bv)
        scores = jnp.einsum('bhqd,bhkd->bhqk', qh, kh) / jnp.sqrt(jnp.float32(D_K))
        sq, sk = (scores.shape[-2], scores.shape[-1])
        if causal_attention:
            causal = jnp.triu(jnp.ones((sq, sk), dtype=bool), k=1)
            scores = jnp.where(causal[None, None], NEG_INF, scores)
        scores = jnp.where(k_mask[:, None, None, :] == 0, NEG_INF, scores)
        attn = jax.nn.softmax(scores, axis=-1)
        attn = jnp.where(q_mask[:, None, :, None] == 0, 0.0, attn)
        out = jnp.einsum('bhqk,bhkd->bhqd', attn, vh)
        out = out.transpose(0, 2, 1, 3).reshape(q.shape[0], sq, D_MODEL)
        return out @ Wo.T + bo

    def _L0_ffn_ref(x, base_w, base_b, lora_A, lora_B, router_w, router_b):
        import jax, jax.numpy as jnp
        import numpy as np
        B, S, D, O, E, R, TOP_K = (4, 128, 128, 128, 8, 16, 2)
        SCALING = 32.0 / 16.0
        NEG_INF = -1000000000.0
        result = jnp.einsum('bsd,od->bso', x, base_w) + base_b
        ax = jnp.einsum('bsd,edr->bser', x, lora_A)
        bax = jnp.einsum('bser,ero->bseo', ax, lora_B)
        logits = jnp.einsum('bsd,ed->bse', x, router_w) + router_b
        kth = jax.lax.top_k(logits, TOP_K)[0][..., -1:]
        masked = jnp.where(logits < kth, NEG_INF, logits)
        expert_weights = jax.nn.softmax(masked, axis=-1)
        return result + SCALING * jnp.einsum('bse,bseo->bso', expert_weights, bax)

    def _L1_xattn_ref(q, k, v, Wq, Wk, Wv, bv, Wo, bo):
        import jax, jax.numpy as jnp
        import numpy as np
        EMBED_PHI = 128
        EMBED_F = 128
        HIDDEN_F = 128
        N_HEADS = 16
        B, S = (2, 256)
        Bq, Sq, _ = q.shape
        hd = HIDDEN_F // N_HEADS
        scale = 1.0 / np.sqrt(hd)
        qh = (q @ Wq.T).reshape(Bq, Sq, N_HEADS, hd).transpose(0, 2, 1, 3)
        kh = (k @ Wk.T).reshape(Bq, Sq, N_HEADS, hd).transpose(0, 2, 1, 3)
        vh = (v @ Wv.T + bv).reshape(Bq, Sq, N_HEADS, hd).transpose(0, 2, 1, 3)
        scores = jnp.einsum('bhsd,bhtd->bhst', qh, kh) * scale
        mask = jnp.triu(jnp.ones((Sq, Sq), dtype=bool), k=0).at[0, 0].set(False)
        scores = jnp.where(mask, -jnp.inf, scores)
        probs = jax.nn.softmax(scores, axis=-1)
        out = jnp.einsum('bhst,bhtd->bhsd', probs, vh)
        out = out.transpose(0, 2, 1, 3).reshape(Bq, Sq, HIDDEN_F)
        return out @ Wo.T + bo

    def _L1_ffn_ref(hidden_states, router_w, e_bias, Wg, Wu, Wd, SWg, SWu, SWd):
        import jax, jax.numpy as jnp
        import numpy as np
        H = 128
        I = 64
        E = 64
        G = 8
        TOPK_GROUP = 4
        K = 8
        I_SH = 128
        SCALE = 2.5

        def _route(x, router_w, e_bias):
            T = x.shape[0]
            scores = jax.nn.sigmoid(x.astype(jnp.float32) @ router_w.T.astype(jnp.float32))
            sfc = jax.lax.stop_gradient(scores) + e_bias[None, :]
            group_scores = jax.lax.top_k(sfc.reshape(T, G, E // G), 2)[0].sum(-1)
            _, gidx = jax.lax.top_k(group_scores, TOPK_GROUP)
            gmask = jax.nn.one_hot(gidx, G, dtype=sfc.dtype).sum(1)
            smask = jnp.repeat(gmask, E // G, axis=1)
            masked = jnp.where(smask > 0, sfc, 0.0)
            _, topk_idx = jax.lax.top_k(masked, K)
            w = jnp.take_along_axis(scores, topk_idx, axis=1)
            w = w / (w.sum(-1, keepdims=True) + 1e-20)
            return (topk_idx, w * SCALE)
        orig_shape = hidden_states.shape
        x = hidden_states.reshape(-1, orig_shape[-1])
        T = x.shape[0]
        topk_idx, topk_w = _route(x, router_w, e_bias)
        coef = jnp.zeros((T, E), topk_w.dtype).at[jnp.arange(T)[:, None], topk_idx].add(topk_w)
        g = jnp.einsum('th,ehi->tei', x, Wg)
        u = jnp.einsum('th,ehi->tei', x, Wu)
        h = jax.nn.silu(g) * u * coef[:, :, None]
        moe_out = jnp.einsum('tei,eih->th', h, Wd)
        shared = jax.nn.silu(x @ SWg) * (x @ SWu) @ SWd
        return (moe_out + shared).reshape(orig_shape)

    def _L2_xattn_ref(q, k, v, mask, w_q, w_k, w_v, w_o):
        import jax, jax.numpy as jnp
        import numpy as np
        import math
        B, S, D, H = (2, 256, 128, 16)
        DK = D // H

        def _split_heads(x):
            b, s, _ = x.shape
            return x.reshape(b, s, H, DK).transpose(0, 2, 1, 3)
        query = _split_heads(q @ w_q.T)
        key = _split_heads(k @ w_k.T)
        value = _split_heads(v @ w_v.T)
        scores = jnp.einsum('bhqd,bhkd->bhqk', query, key) / math.sqrt(DK)
        scores = jnp.where(mask[:, None, None, :] == 0, jnp.float32(-1000000000.0), scores)
        attn = jax.nn.softmax(scores, axis=-1)
        mh_out = jnp.einsum('bhqk,bhkd->bhqd', attn, value)
        mh_out = mh_out.transpose(0, 2, 1, 3).reshape(q.shape[0], -1, D)
        return mh_out @ w_o.T

    def _L2_ffn_ref(h, router_w, w1, b1, w2, b2):
        import jax, jax.numpy as jnp
        import numpy as np
        B, S, D, E, F = (2, 256, 128, 14, 256)
        Bb, Ss, Dd = h.shape
        x = h.reshape(-1, Dd)
        logits = x @ router_w
        assignments = jnp.argmax(logits, axis=-1)
        probs = jax.nn.softmax(logits, axis=-1)
        weights = jnp.take_along_axis(probs, assignments[:, None], axis=1)[:, 0]
        hid = jnp.einsum('nd,edf->nef', x, w1) + b1
        hid = jax.nn.gelu(hid, approximate=False)
        all_out = jnp.einsum('nef,efd->ned', hid, w2) + b2
        sel = jnp.take_along_axis(all_out, assignments[:, None, None], axis=1)[:, 0, :]
        moe_out = (sel * weights[:, None]).reshape(Bb, Ss, Dd)
        return moe_out

    def _L3_xattn_ref(Q, K, V, Wq, Wk, Wv, Wo, bq, bk, bv, bo):
        import jax, jax.numpy as jnp
        import numpy as np
        EMBED = 128
        HEADS = 16
        HEAD_DIM = EMBED // HEADS
        B, S, E = Q.shape
        H, Dh = (HEADS, HEAD_DIM)
        q = (Q @ Wq.T + bq).reshape(B, S, H, Dh).transpose(0, 2, 1, 3)
        k = (K @ Wk.T + bk).reshape(B, S, H, Dh).transpose(0, 2, 1, 3)
        v = (V @ Wv.T + bv).reshape(B, S, H, Dh).transpose(0, 2, 1, 3)
        A = jnp.einsum('bhqd,bhkd->bhqk', q, k) / np.sqrt(Dh).astype(np.float32)
        causal = jnp.tril(jnp.ones((S, S), dtype=bool))
        A = jnp.where(causal, A, -jnp.inf)
        w = jax.nn.softmax(A, axis=-1)
        out = jnp.einsum('bhqk,bhkd->bhqd', w, v)
        out = out.transpose(0, 2, 1, 3).reshape(B, S, E)
        return out @ Wo.T + bo

    def _L3_ffn_ref(hidden_states, q_w, q_b, k_w, k_b, v_w, v_b, o_w, o_b, router_w, router_b, w1, b1, w2, b2):
        import jax, jax.numpy as jnp
        import numpy as np
        import math
        D = 128
        H = 16
        E = 8
        TOPK = 2
        LAT = D // 2
        KPH = LAT // H
        HD = D // H

        def _forward(hs, q_w, q_b, k_w, k_b, v_w, v_b, o_w, o_b, router_w, router_b, w1, b1, w2, b2):
            B, S, _ = hs.shape
            Q = (hs @ q_w + q_b).reshape(B, S, H, HD).transpose(0, 2, 1, 3)
            K = (hs @ k_w + k_b).reshape(B, S, H, KPH).transpose(0, 2, 1, 3)
            V = (hs @ v_w + v_b).reshape(B, S, H, KPH).transpose(0, 2, 1, 3)
            scores = jnp.einsum('bhsk,bhtk->bhst', Q[..., :KPH], K) / math.sqrt(KPH)
            attn = jax.nn.softmax(scores, axis=-1)
            ao = jnp.einsum('bhst,bhtv->bhsv', attn, V)
            ao = ao.transpose(0, 2, 1, 3).reshape(B, S, H * KPH)
            ao = jnp.concatenate([ao, jnp.zeros((B, S, D - LAT), ao.dtype)], axis=-1)
            mla_out = ao @ o_w + o_b
            probs = jax.nn.softmax(mla_out @ router_w + router_b, axis=-1)
            topw, topi = jax.lax.top_k(probs, TOPK)
            topw = topw / (topw.sum(-1, keepdims=True) + 1e-08)
            combine = jnp.sum(jax.nn.one_hot(topi, E, dtype=probs.dtype) * topw[..., None], axis=-2)
            h1 = jnp.einsum('bsd,edf->ebsf', mla_out, w1) + b1[:, None, None, :]
            h1 = jax.nn.gelu(h1, approximate=False)
            h2 = jnp.einsum('ebsf,efd->ebsd', h1, w2) + b2[:, None, None, :]
            moe_out = jnp.einsum('bse,ebsd->bsd', combine, h2)
            return hs + 0.3 * moe_out
        return _forward(hidden_states, q_w, q_b, k_w, k_b, v_w, v_b, o_w, o_b, router_w, router_b, w1, b1, w2, b2)
    x = x + jnp.tanh(g_xattn[0]) * _L0_xattn_ref(_layernorm(x, axis=-1), ctx_1024, mask_BxS2_ik0, mask_BxS2_ik0, L0_xattn_Wq, L0_xattn_bq, L0_xattn_Wk, L0_xattn_bk, L0_xattn_Wv, L0_xattn_bv, L0_xattn_Wo, L0_xattn_bo, 1)
    x = x + jnp.tanh(g_ffn[0]) * _L0_ffn_ref(_layernorm(x, axis=-1), L0_ffn_base_w, L0_ffn_base_b, L0_ffn_lora_A, L0_ffn_lora_B, L0_ffn_router_w, L0_ffn_router_b)
    x = x + jnp.tanh(g_xattn[1]) * _L1_xattn_ref(_layernorm(x, axis=-1), ctx_1024, ctx_1024, L1_xattn_Wq, L1_xattn_Wk, L1_xattn_Wv, L1_xattn_bv, L1_xattn_Wo, L1_xattn_bo)
    x = x + jnp.tanh(g_ffn[1]) * _L1_ffn_ref(_layernorm(x, axis=-1), L1_ffn_router_w, L1_ffn_e_bias, L1_ffn_Wg, L1_ffn_Wu, L1_ffn_Wd, L1_ffn_SWg, L1_ffn_SWu, L1_ffn_SWd)
    x = x + jnp.tanh(g_xattn[2]) * _L2_xattn_ref(_layernorm(x, axis=-1), ctx_1024, ctx_1024, mask_BxS2_ik0, L2_xattn_w_q, L2_xattn_w_k, L2_xattn_w_v, L2_xattn_w_o)
    x = x + jnp.tanh(g_ffn[2]) * _L2_ffn_ref(_layernorm(x, axis=-1), L2_ffn_router_w, L2_ffn_w1, L2_ffn_b1, L2_ffn_w2, L2_ffn_b2)
    x = x + jnp.tanh(g_xattn[3]) * _L3_xattn_ref(_layernorm(x, axis=-1), ctx_1024, ctx_1024, L3_xattn_Wq, L3_xattn_Wk, L3_xattn_Wv, L3_xattn_Wo, L3_xattn_bq, L3_xattn_bk, L3_xattn_bv, L3_xattn_bo)
    x = x + jnp.tanh(g_ffn[3]) * _L3_ffn_ref(_layernorm(x, axis=-1), L3_ffn_q_w, L3_ffn_q_b, L3_ffn_k_w, L3_ffn_k_b, L3_ffn_v_w, L3_ffn_v_b, L3_ffn_o_w, L3_ffn_o_b, L3_ffn_router_w, L3_ffn_router_b, L3_ffn_w1, L3_ffn_b1, L3_ffn_w2, L3_ffn_b2)
    return x

_drawn_inputs = setup_inputs


def setup_inputs(seed=0):
    import zlib

    import numpy as np

    out = dict(_drawn_inputs(seed))
    spreads = {'L0_xattn_bq': (0.0, 0.8),
     'L0_xattn_bk': (0.0, 2.0),
     'L0_xattn_bv': (0.0, 0.367),
     'L0_xattn_bo': (0.0, 0.1),
     'L0_ffn_base_b': (0.0, 0.1),
     'L0_ffn_router_b': (0.0, 0.662),
     'L1_ffn_e_bias': (0.0, 0.8),
     'L2_ffn_b1': (0.0, 2.0),
     'L2_ffn_b2': (0.0, 2.0),
     'L3_ffn_q_b': (0.0, 0.8),
     'L3_ffn_k_b': (0.0, 2.0),
     'L3_ffn_v_b': (0.0, 0.8),
     'L3_ffn_o_b': (0.0, 0.8),
     'L3_ffn_router_b': (0.0, 0.8),
     'L3_ffn_b1': (0.0, 0.8),
     'L3_ffn_b2': (0.0, 0.8)}
    factors = {'g_ffn': 26.792,
     'L0_ffn_lora_A': 2.783,
     'L0_ffn_lora_B': 2.818,
     'L0_ffn_router_w': 3.169,
     'L1_ffn_router_w': 8.0,
     'L1_ffn_Wg': 8.0,
     'L1_ffn_Wu': 8.0,
     'L1_ffn_Wd': 8.0,
     'L1_ffn_SWg': 7.872,
     'L1_ffn_SWu': 7.919,
     'L1_ffn_SWd': 7.998,
     'L3_xattn_bq': 62.606,
     'L3_xattn_bk': 64.0,
     'L3_xattn_bv': 24.722,
     'L3_xattn_bo': 25.252,
     'L3_ffn_q_w': 8.0,
     'L3_ffn_k_w': 8.0,
     'L3_ffn_v_w': 8.0,
     'L3_ffn_o_w': 8.0,
     'L3_ffn_router_w': 8.0,
     'L3_ffn_w1': 8.0,
     'L3_ffn_w2': 8.0}
    for name, (base, spread) in spreads.items():
        noise = np.random.default_rng([zlib.crc32(name.encode()), seed]).standard_normal(out[name].shape)
        drawn = base * np.exp(spread * noise) if base else spread * noise
        out[name] = jnp.asarray(drawn.astype(out[name].dtype))
    for name, factor in factors.items():
        out[name] = (out[name] * factor).astype(out[name].dtype)
    return out
```

```python
from contextlib import ExitStack

import concourse.bass as bass
from concourse import mybir

F32 = mybir.dt.float32
F16 = mybir.dt.float16
BF16 = mybir.dt.bfloat16
I32 = mybir.dt.int32
ACT = mybir.ActivationFunctionType
ALU = mybir.AluOpType
AX = mybir.AxisListType

P = 128
B, S, D = 8, 256, 128
T = B * S
NT = T // P
CH = 512
NC = T // CH
H, DH = 16, 8
EPS = 1e-5
HU = 8
NU = B * H // HU
RT = 6 * DH
RB = RT + 3
RM = RB + 3
BIG = float(2.0 ** 100)
Q_PARTS = (0, 0, 0, 1, 1, 2)
K_PARTS = (0, 1, 2, 0, 1, 0)
VW = 3 * DH + 1

ATT = [
    dict(causal="incl", keymask=True, dk=8, dv=8, gate=0),
    dict(causal="strict", keymask=False, dk=8, dv=8, gate=1),
    dict(causal=None, keymask=True, dk=8, dv=8, gate=2),
    dict(causal="incl", keymask=False, dk=8, dv=8, gate=3),
    dict(causal=None, keymask=False, dk=4, dv=4, gate=None),
]
MOE = [
    dict(E=8, J=1, f=ACT.Identity),
    dict(E=64, J=32, f=ACT.Silu),
    dict(E=14, J=28, f=ACT.Gelu),
    dict(E=8, J=16, f=ACT.Gelu),
]
W_OFF, n = {}, 0
for _l in range(5):
    for _k in "qkvo":
        W_OFF[_k, _l] = n
        n += D
for _k in ("base", "loraA", "loraB"):
    W_OFF[_k] = n
    n += D
for _l in range(4):
    W_OFF["r", _l] = n
    n += MOE[_l]["E"]
W_N = n
C_OFF, n = {}, 0
for _l in range(5):
    for _k in "qk":
        C_OFF[_k, _l] = n
        n += 1
C_OFF["base"] = n
C_OFF["b1", 2] = n + 1
C_OFF["b1", 3] = n + 1 + 28
C_OFF["zero"] = n + 1 + 28 + 16
C_OFF["o", 4] = C_OFF["zero"] + 3
C_OFF["cmask", 0] = C_OFF["zero"] + 1
C_OFF["cmask", 2] = C_OFF["zero"] + 2
C_N = C_OFF["zero"] + 4
R_OFF, n = {}, 0
for _l in range(5):
    for _k in "vo":
        R_OFF[_k, _l] = n
        n += D
for _k, _w in (("base", D), (("r", 0), 8), (("r", 3), 8), ("ebias", 64), ("g", 8)):
    R_OFF[_k] = n
    n += _w
R_N = n
SEL_OFF = {0: 0, 1: 128, 2: 128 + 32 * 128, 3: 128 + 32 * 128 + 14 * 128}
SEL_N = 128 * (1 + 32 + 14 + 8)
WF = 3 * 33 * 128


def build(nc, dr, out):
    with ExitStack() as ctx:
        def sb(name, shape, dt=F32):
            return ctx.enter_context(nc.sbuf_tensor(name, shape, dt))

        def sem(name):
            return ctx.enter_context(nc.semaphore(name))

        ps = ctx.enter_context(nc.psum_tensor("ps", [P, 8, CH], F32))
        x = sb("x", [P, NT * D])
        xn = sb("xn", [P, NT * D])
        xnT = sb("xnT", [P, T])
        ctxT = sb("ctxT", [P, T])
        ao = sb("ao", [P, NT * D])
        xh = ao[:].bitcast(F16).rearrange("p (a t) -> p a t", a=2)
        wp = sb("wp", [P, W_N])
        wf = sb("wf", [P, WF])
        cols = sb("cols", [P, C_N])
        rows = sb("rows", [P, R_N])
        b2 = sb("b2", [28, 2, D])
        b2h = sb("b2h", [28, 2, 2, D], F16)
        ident = sb("ident", [P, P])
        identb = sb("identb", [P, P], BF16)
        identh = sb("identh", [P, P], F16)
        maskb = sb("maskb", [P, 3, P], BF16)
        maskf = sb("maskf", [P, 3, P])
        sel = sb("sel", [P, SEL_N], F16)
        keep = sb("keep", [P, T], BF16)
        qkeep = sb("qkeep", [P, NT])
        ones = sb("ones", [P, NT])
        gate = sb("gate", [P, 8])
        V = sb("V", [P, NT, H, VW], BF16)
        stats = sb("stats", [P, NT, 6])
        mom = sb("mom", [P, 6, NT])
        rstd = sb("rstd", [P, NT])
        neghalf = sb("neghalf", [P, NT])
        qb = sb("qb", [P, 5])
        top = sb("top", [P, NT, 8])
        small = sb("small", [P, 4, NT, 8])
        coefT = sb("coefT", [P, T], F16)
        Qs = sb("Qs", [RM, 4, HU, S], BF16)
        Ks = sb("Ks", [RM, 4, HU, S], BF16)
        work = sb("work", [P, 5248])
        kf = work[:, 0:1024].rearrange("p (k c) -> p k c", k=2)
        rem = work[:, 1024:2048].rearrange("p (k c) -> p k c", k=2)
        parts = work[:, 2048:3584].bitcast(BF16).rearrange("p (k a c) -> p k a c", k=2, a=3)
        biasrow = work[0:48, 3584:4608].bitcast(BF16)
        vf = work[:, 4608:5120]
        prob = work[:, 0:2048].rearrange("p (r i c) -> p r i c", r=2, i=2)
        probhi = work[:, 0:2048].bitcast(BF16).rearrange("p (r i c two) -> p r i two c", r=2, i=2, two=2)[:, :, :, 1]
        problo = work[:, 2048:3072].bitcast(F16).rearrange("p (r i c) -> p r i c", r=2, i=2)
        rt = work[:, 0:4096].rearrange("p (r t e) -> p r t e", r=4, t=NT)
        coef = work[:, 4224:5248].bitcast(F16).rearrange("p (t e) -> p t e", t=NT)
        hid = work[:, 0:2048].rearrange("p (r k c) -> p r k c", r=2, k=2)
        whi = work[:, 0:4224].bitcast(F16)
        bmax = sb("bmax", [P, HU, 3])
        nmax = sb("nmax", [P, 3, 2, HU])
        nparts = sb("nparts", [P, 2, 3, HU], BF16)
        nmT = sb("nmT", [24, 2, S], BF16)
        rsum = sb("rsum", [P, 2 * HU])
        osum = sb("osum", [P, 2 * HU, DH])

        scrQ = nc.dram_tensor("scrQ", [RT, H, T], BF16, kind="Internal").ap()
        scrK = nc.dram_tensor("scrK", [RB, H, T], BF16, kind="Internal").ap()
        scrM = nc.dram_tensor("scrM", [2, 24, S], BF16, kind="Internal").ap()

        wsem = [sem(f"experts_loaded{l}") for l in range(4)]
        s_out = sem("s_out")
        st = dict(locals())
        sem = StageSemaphores(nc)
        setup_stage(nc, st, dr, sem)
        for l in range(4):
            project_stage(nc, st, sem, l, l)
            attend_stage(nc, st, sem, l, dr)
            output_stage(nc, st, sem, l)
            if l == 3:
                norm_stage(nc, st, sem, "n3")
                project_stage(nc, st, sem, 4, 4)
                attend_stage(nc, st, sem, 4, dr)
                output_stage(nc, st, sem, 4)
            route_stage(nc, st, sem, l, dr)
            expert_stage(nc, st, sem, l)
        with nc.Block() as block:
            @block.sync
            def _(sp):
                sp.dma_start(out.rearrange("b (t p) d -> p (b t) d", p=P),
                             x[:].rearrange("p (t d) -> p t d", d=D)).then_inc(s_out, 16)
                sp.wait_ge(s_out, 16)


class StageSemaphores:
    COUNT = 32

    def __init__(self, nc):
        free = sorted(nc.free_semaphores)
        self.nc, self.turn, self.open, self.used = nc, 0, [], 0
        self.first = []
        for n in free:
            if all(n + i in free for i in range(2 * self.COUNT)):
                self.first = [n, n + self.COUNT]
                break

    def next_stage(self):
        for s in self.open:
            self.nc.release_semaphore(s)
        last = range(self.first[self.turn], self.first[self.turn] + self.COUNT)
        self.open, self.used, self.turn = [], 0, 1 - self.turn
        return last

    def __call__(self, name):
        assert self.used < self.COUNT
        s = self.nc.alloc_semaphore(name=name, num=self.first[self.turn] + self.used)
        self.used += 1
        self.open.append(s)
        return s


def wait_apart(sp, semaphore, value, passed):
    sp.wait_ge(semaphore, value)
    sp.sem_inc(passed, 1)


def bc(ap, shape):
    return ap.to_broadcast(shape)


def setup_stage(nc, st, dr, sem):
    ps, x, wp, cols, rows, b2 = (st[k] for k in ("ps", "x", "wp", "cols", "rows", "b2"))
    ao, ctxT, ident = st["ao"], st["ctxT"], st["ident"]
    maski = st["xnT"][:].bitcast(I32)
    qmaski = st["stats"][:].rearrange("p a b -> p (a b)").bitcast(I32)[:, 0:NT]
    s_in = sem("set_loaded")
    s_ctx = sem("set_ctx_loaded")
    s_t = sem("set_transposed")
    s_ms = sem("set_constants")
    with nc.Block() as block:
        @block.sync
        def _(sp):
            sp.dma_start(ao[:].rearrange("p (t d) -> p t d", d=D),
                         dr["ctx"].rearrange("b (t p) d -> p (b t) d", p=P)).then_inc(s_ctx, 16)
            sp.dma_start(ident[:], dr["ident"]).then_inc(s_ctx, 16)
            sp.dma_start(x[:].rearrange("p (t d) -> p t d", d=D),
                         dr["x"].rearrange("b (t p) d -> p (b t) d", p=P)).then_inc(s_in, 16)
            sp.dma_start(wp[:], dr["wpack"]).then_inc(s_in, 16)
            sp.dma_start(cols[:], dr["cols"]).then_inc(s_in, 16)
            sp.dma_start(rows[:], dr["rows"].partition_broadcast(P)).then_inc(s_in, 16)
            sp.dma_start(b2[:], dr["b2"].rearrange("a e d -> e a d")).then_inc(s_in, 16)
            sp.dma_start(maski, dr["mask"].rearrange("b s -> (b s)").partition_broadcast(P)).then_inc(s_in, 16)
            with nc.allow_non_contiguous_dma(reason="one mask value a descriptor, 2048 of them once"):
                sp.dma_start(qmaski, dr["mask"].rearrange("b (t p) -> p (b t)", p=P)).then_inc(s_in, 16)
            sp.dma_start(st["maskf"][:], dr["causal"]).then_inc(s_in, 16)
            sp.dma_start(st["sel"][:], dr["sel"]).then_inc(s_in, 16)

        @block.tensor
        def _(pe):
            pe.wait_ge(s_ctx, 32)
            for c in range(NC):
                for k in range(4):
                    t = 4 * c + k
                    ins = pe.transpose(ps[:, c, k * P:(k + 1) * P], ao[:, t * D:(t + 1) * D], ident[:])
                ins.then_inc(s_t, 1)

        @block.scalar
        def _(act):
            for c in range(NC):
                act.wait_ge(s_t, c + 1)
                act.copy(ctxT[:, c * CH:(c + 1) * CH], ps[:, c, :])
            act.wait_ge(s_in, 144)
            act.activation(st["gate"][:], rows[:, R_OFF["g"]:R_OFF["g"] + 8], ACT.Tanh)

        @block.vector
        def _(dve):
            dve.memset(st["V"][:], 1.0)
            dve.memset(st["ones"][:], 1.0)
            dve.memset(st["neghalf"][:], -0.5)
            dve.memset(st["Qs"][:], 1.0)
            dve.memset(st["Ks"][:], 1.0)
            dve.wait_ge(s_ctx, 32)
            dve.tensor_copy(st["identb"][:], ident[:])
            dve.tensor_copy(st["identh"][:], ident[:])
            dve.wait_ge(s_in, 144)
            dve.tensor_copy(st["maskb"][:], st["maskf"][:])
            dve.tensor_copy(st["b2h"][:, 0], b2[:])
            dve.drain()
            dve.tensor_tensor(st["b2h"][:, 1], b2[:], st["b2h"][:, 0], ALU.subtract)
            dve.tensor_scalar(st["keep"][:], maski, 0.0, None, ALU.not_equal)
            dve.tensor_scalar(st["qkeep"][:], qmaski, 0.0, None, ALU.not_equal)
            for a in range(5):
                dve.tensor_scalar(st["qb"][:, a:a + 1], cols[:, C_OFF["q", a]:C_OFF["q", a] + 1],
                                  float(ATT[a]["dk"]) ** -0.5, None, ALU.mult)


def norm_vector(nc, st, dve, s_var, s_rstd, s_xn):
    x, xn, stats, mom = st["x"], st["xn"], st["stats"], st["mom"]
    with dve.Fori(0, NT) as t:
        dve.bn_stats(stats[:].rearrange("p t s -> p (t s)")[:, bass.ds(t * 6, 6)], x[:, bass.ds(t * D, D)])
    dve.drain()
    dve.tensor_tensor(mom[:, 0, :], stats[:, :, 1], stats[:, :, 4], ALU.add)
    dve.tensor_tensor(mom[:, 1, :], stats[:, :, 1], stats[:, :, 4], ALU.subtract)
    dve.tensor_tensor(mom[:, 2, :], stats[:, :, 2], stats[:, :, 5], ALU.add)
    dve.drain()
    dve.tensor_tensor(mom[:, 3, :], mom[:, 1, :], mom[:, 1, :], ALU.mult)
    dve.tensor_scalar(mom[:, 4, :], mom[:, 0, :], 0.5, None, ALU.mult)
    dve.tensor_scalar(mom[:, 2, :], mom[:, 2, :], 1.0 / D, EPS, ALU.mult, ALU.add)
    dve.drain()
    dve.scalar_tensor_tensor(mom[:, 5, :], mom[:, 3, :], 0.25, mom[:, 2, :], ALU.mult, ALU.add).then_inc(s_var, 1)
    dve.wait_ge(s_rstd, 1)
    for c in range(NC):
        sl = slice(4 * c, 4 * c + 4)
        xc = x[:, c * CH:(c + 1) * CH].rearrange("p (t d) -> p t d", d=D)
        yc = xn[:, c * CH:(c + 1) * CH].rearrange("p (t d) -> p t d", d=D)
        dve.tensor_tensor(yc, xc, bc(mom[:, 4, sl].rearrange("p (t o) -> p t o", o=1), [P, 4, D]), ALU.subtract)
        dve.drain()
        dve.tensor_tensor(yc, yc, bc(st["rstd"][:, sl].rearrange("p (t o) -> p t o", o=1), [P, 4, D]),
                          ALU.mult).then_inc(s_xn, 1)


def norm_pool(nc, st, pool, s_var, s_rstd):
    pool.wait_ge(s_var, 1)
    pool.tensor_tensor(st["rstd"][:], st["mom"][:, 5, :], st["neghalf"][:], ALU.pow).then_inc(s_rstd, 1)


def norm_tensor(nc, st, pe, s_xn, s_xt, bank0):
    for c in range(NC):
        pe.wait_ge(s_xn, c + 1)
        for k in range(4):
            t = 4 * c + k
            ins = pe.transpose(st["ps"][:, bank0 + c, k * P:(k + 1) * P], st["xn"][:, t * D:(t + 1) * D],
                               st["ident"][:])
        ins.then_inc(s_xt, 1)


def norm_scalar(nc, st, act, s_xt, s_xc, bank0):
    for c in range(NC):
        act.wait_ge(s_xt, c + 1)
        act.copy(st["xnT"][:, c * CH:(c + 1) * CH], st["ps"][:, bank0 + c, :]).then_inc(s_xc, 1)


def norm_stage(nc, st, sem, tag):
    ended = sem.next_stage()
    s_var, s_rstd, s_xn, s_xt, s_xc = (sem(f"{tag}_{k}") for k in ("var", "rstd", "xn", "xt", "xc"))
    with nc.Block() as block:
        @block.vector
        def _(dve):
            norm_vector(nc, st, dve, s_var, s_rstd, s_xn)

        @block.gpsimd
        def _(pool):
            pool.sem_clear(ended)
            norm_pool(nc, st, pool, s_var, s_rstd)

        @block.tensor
        def _(pe):
            norm_tensor(nc, st, pe, s_xn, s_xt, 4)

        @block.scalar
        def _(act):
            norm_scalar(nc, st, act, s_xt, s_xc, 4)


def project_stage(nc, st, sem, a, l):
    ended = sem.next_stage()
    own = a == 4
    ps, wp, cols, rows, V, vf = (st[k] for k in ("ps", "wp", "cols", "rows", "V", "vf"))
    kf, rem, parts = st["kf"], st["rem"], st["parts"]
    src = st["xnT"] if own else st["ctxT"]
    att = ATT[a]
    s_var, s_rstd, s_xn, s_xt, s_xc = (sem(f"p{a}_{k}") for k in ("var", "rstd", "xn", "xt", "xc"))
    s_pj, s_kf, s_parts, s_v, s_vf, s_vp = (
        sem(f"p{a}_{k}") for k in ("projected", "evacuated", "parts", "v", "vcopied", "vparts"))
    s_wr = [sem(f"p{a}_written{k}") for k in range(2)]
    s_bias = sem(f"p{a}_bias")
    passed = sem(f"p{a}_passed")
    s_biasw = sem(f"p{a}_biaswritten")

    def w(k):
        o = W_OFF[k, a]
        return wp[:, o:o + D]

    with nc.Block() as block:
        @block.tensor
        def _(pe):
            def project(which, data, first):
                with pe.Fori(0, NC // 2) as i:
                    for k in range(2):
                        pe.wait_ge(s_kf, i * 2 + (first + k + 1))
                        pe.matmul(ps[:, k, :], w(which), data[:, bass.ds(i * 2 * CH + k * CH, CH)],
                                  start=True, stop=True).then_inc(s_pj, 1)
            project("k", src, 0)
            for c in range(NC):
                if c >= 2:
                    pe.wait_ge(s_vf, c - 1)
                for k in range(4):
                    t = 4 * c + k
                    ins = pe.matmul(ps[:, 2 + c % 2, k * P:(k + 1) * P], src[:, t * P:(t + 1) * P], w("v"),
                                    start=True, stop=True)
                ins.then_inc(s_v, 1)
            if not own:
                norm_tensor(nc, st, pe, s_xn, s_xt, 4)
                pe.wait_ge(s_xc, NC)
            project("q", st["xnT"], NC)

        @block.scalar
        def _(act):
            act.sem_inc(s_kf, 2)

            def evacuate(which, first):
                bias = st["qb"][:, a:a + 1] if which == "q" else cols[:, C_OFF["k", a]:C_OFF["k", a] + 1]
                scale = float(att["dk"]) ** -0.5 if which == "q" else 1.0
                with act.Fori(0, NC // 2) as i:
                    for k in range(2):
                        act.wait_ge(s_pj, i * 2 + (first + k + 1))
                        act.wait_ge(s_parts, i * 2 + (first + k + 1))
                        act.activation(kf[:, k, :], ps[:, k, :], ACT.Identity, bias=bias,
                                       scale=scale).then_inc(s_kf, 1)
            evacuate("k", 0)
            if not own:
                norm_scalar(nc, st, act, s_xt, s_xc, 4)
            evacuate("q", NC)

        @block.gpsimd
        def _(pool):
            pool.sem_clear(ended)
            for c in range(NC):
                v3 = vf.rearrange("p (t h d) -> p t h d", t=4, h=H)
                part = [V[:, 4 * c:4 * c + 4, :, i * DH:(i + 1) * DH] for i in range(3)]
                pool.wait_ge(s_vf, c + 1)
                pool.tensor_copy(part[0], v3)
                pool.drain()
                pool.tensor_tensor(v3, v3, part[0], ALU.subtract)
                pool.drain()
                pool.tensor_copy(part[1], v3)
                pool.drain()
                pool.tensor_tensor(part[2], v3, part[1], ALU.subtract).then_inc(s_vp, 1)
            if not own:
                norm_pool(nc, st, pool, s_var, s_rstd)

        @block.vector
        def _(dve):
            dve.sem_inc(s_parts, 2)
            if att["keymask"]:
                cm = cols[0:48, C_OFF["cmask", a]:C_OFF["cmask", a] + 1]
                dve.tensor_scalar(st["biasrow"], st["keep"][0:48, :], 1.0, cm, ALU.subtract,
                                  ALU.mult).then_inc(s_bias, 1)
            else:
                dve.memset(st["biasrow"], 0.0).then_inc(s_bias, 1)

            def split(which, first):
                with dve.Fori(0, NC // 2) as i:
                    for k in range(2):
                        dve.wait_ge(s_kf, i * 2 + (first + k + 3))
                        if which == "k" and att["keymask"]:
                            dve.tensor_tensor(kf[:, k, :], kf[:, k, :],
                                              st["keep"][:, bass.ds(i * 2 * CH + k * CH, CH)], ALU.mult)
                            dve.drain()
                        dve.wait_ge(s_wr[k], i * 96 + 96 * (first // 2 + 1))
                        dve.tensor_copy(parts[:, k, 0, :], kf[:, k, :])
                        dve.drain()
                        dve.tensor_tensor(rem[:, k, :], kf[:, k, :], parts[:, k, 0, :], ALU.subtract)
                        dve.drain()
                        dve.tensor_copy(parts[:, k, 1, :], rem[:, k, :])
                        dve.drain()
                        dve.tensor_tensor(parts[:, k, 2, :], rem[:, k, :], parts[:, k, 1, :],
                                          ALU.subtract).then_inc(s_parts, 1)
            split("k", 0)
            for c in range(NC):
                dve.wait_ge(s_v, c + 1)
                if c >= 1:
                    dve.wait_ge(s_vp, c)
                dve.tensor_tensor(
                    vf.rearrange("p (t d) -> p t d", t=4),
                    ps[:, 2 + c % 2, :].rearrange("p (t d) -> p t d", t=4),
                    bc(rows[:, R_OFF["v", a]:R_OFF["v", a] + D].rearrange("p (o d) -> p o d", o=1), [P, 4, D]),
                    ALU.add).then_inc(s_vf, 1)
            if not own:
                norm_vector(nc, st, dve, s_var, s_rstd, s_xn)
            split("q", NC)

        @block.sync
        def _(sp):
            for k in range(2):
                sp.sem_inc(s_wr[k], 96)
            sp.wait_ge(s_bias, 1)
            sp.dma_start(st["scrK"][RT:RB].rearrange("a h t -> (a h) t"), st["biasrow"]).then_inc(s_biasw, 16)

            def write(scr, order, first):
                with sp.Fori(0, NC // 2) as i:
                    for k in range(2):
                        at = sp.snap(i * 2 * CH + k * CH)
                        wait_apart(sp, s_parts, i * 2 + (first + k + 3), passed)
                        for g, part in enumerate(order):
                            sp.dma_start(scr[DH * g:DH * g + DH, :, bass.ds(at, CH)].rearrange("d h t -> (d h) t"),
                                         parts[:, k, part, :]).then_inc(s_wr[k], 16)
            write(st["scrK"], K_PARTS, 0)
            write(st["scrQ"], Q_PARTS, NC)
            for k in range(2):
                sp.wait_ge(s_wr[k], 96 * (NC + 1))
            sp.wait_ge(s_biasw, 16)



def load_experts(nc, st, sp, s_w, l, dr):
    wf = st["wf"]
    if l == 1:
        n = 33 * P
        for i, k in enumerate(("L1_wg", "L1_wu", "L1_wd")):
            sp.dma_start(wf[:, i * n:(i + 1) * n], dr[k]).then_inc(s_w, 16)
        return 48
    n = MOE[l]["J"] * P
    for i, k in enumerate((f"L{l}_w1", f"L{l}_w2")):
        sp.dma_start(wf[:, i * n:(i + 1) * n], dr[k]).then_inc(s_w, 16)
    return 32


def attend_stage(nc, st, sem, a, dr):
    ended = sem.next_stage()
    att = ATT[a]
    causal = att["causal"]
    ps, Qs, Ks, prob, probhi, problo, V, ao = (
        st[k] for k in ("ps", "Qs", "Ks", "prob", "probhi", "problo", "V", "ao"))
    identb, maskb = st["identb"], st["maskb"]
    bmax, nmax, nparts, nmT, rsum, osum = (st[k] for k in ("bmax", "nmax", "nparts", "nmT", "rsum", "osum"))
    scrQ, scrK, scrM = st["scrQ"], st["scrK"], st["scrM"]
    NB = 3 if causal else 2
    BW = 128 if causal else 256
    W1 = 384 if causal else 512
    m0, m1 = {None: (None, None), "incl": (0, 0), "strict": (2, 1)}[causal]
    loaded = [sem(f"a{a}_loaded{k}") for k in range(4)]
    rows_done = sem(f"a{a}_rows_done")
    rows_read = sem(f"a{a}_rows_read")
    scored = sem(f"a{a}_scored")
    exped = sem(f"a{a}_exped")
    rest0 = sem(f"a{a}_rest0")
    rest1 = sem(f"a{a}_rest1")
    weighted = sem(f"a{a}_weighted")
    normed = sem(f"a{a}_normed")
    maxparts = sem(f"a{a}_maxparts")
    maxout = sem(f"a{a}_max_out")
    passed = sem(f"a{a}_passed")
    maxin = sem(f"a{a}_max_in")

    def lin(it, k, per_unit, base):
        v = per_unit * k + base
        return v + 4 * per_unit * it if isinstance(it, int) else it * (4 * per_unit) + v

    def slots(eng, body):
        with eng.Fori(0, NU // 4 - 1) as it:
            for k in range(4):
                body(it, k)
        for k in range(4):
            body(NU // 4 - 1, k)

    def heads_left(it, k):
        return not isinstance(it, int) or k < 2

    def maxima_left(it, k):
        return not isinstance(it, int) or k < 3

    def rest(eng, it, k, g, i):
        eng.wait_ge(weighted, lin(it, k, 4, g + 1))
        eng.wait_ge(exped, lin(it, k, 4, g + 3))
        eng.tensor_tensor(problo[:, g % 2, i, 0:W1], prob[:, g % 2, i, 0:W1], probhi[:, g % 2, i, 0:W1],
                          ALU.subtract).then_inc((rest0, rest1)[i], 1)

    with nc.Block() as block:
        @block.gpsimd
        def _(pool):
            pool.sem_clear(ended)

            def slot(it, k):
                for g in range(4):
                    rest(pool, it, k, g, 1)
            slots(pool, slot)

        @block.tensor
        def _(pe):
            pe.sem_inc(weighted, 2)

            def head_rows(slot, h, bank, item):
                pe.wait_ge(rows_read, item + 1)
                M = ps[:, bank, :]
                q, kk = Qs[0:RB, slot, h, :], Ks[0:RB, slot, h, :]
                if causal:
                    pe.matmul(M[:, 0:128], q[:, 0:128], kk[:, 0:128], start=True, stop=False)
                    pe.matmul(M[:, 0:128], identb[:], maskb[:, m0, :], start=False, stop=True)
                    pe.matmul(M[:, 128:256], q[:, 128:256], kk[:, 0:128], start=True, stop=True)
                    pe.matmul(M[:, 256:384], q[:, 128:256], kk[:, 128:256], start=True, stop=False)
                    ins = pe.matmul(M[:, 256:384], identb[:], maskb[:, m1, :], start=False, stop=True)
                else:
                    pe.matmul(M[:, 0:256], q[:, 0:128], kk[:, 0:256], start=True, stop=True)
                    ins = pe.matmul(M[:, 256:512], q[:, 128:256], kk[:, 0:256], start=True, stop=True)
                ins.then_inc(rows_done, 1)

            def max_rows(bank, item, unit_plus_1):
                pe.wait_ge(rows_read, item + 1)
                pe.wait_ge(maxparts, unit_plus_1)
                out = ps[:, bank, :].bitcast(BF16)
                for qt in range(2):
                    ins = pe.transpose(out[0:24, qt * 128:qt * 128 + 128],
                                       nparts[:, qt, :, :].rearrange("p a h -> p (a h)"), identb[:])
                ins.then_inc(rows_done, 1)

            def scores(it, k, g):
                pe.wait_ge(exped, lin(it, k, 4, g + 1))
                for i in range(2):
                    h = 2 * g + i
                    O = ps[:, 2 * (g % 2) + i, :]
                    q, kk = Qs[0:RM, k, h, :], Ks[0:RM, k, h, :]
                    if causal:
                        pe.matmul(O[:, 0:128], kk[:, 0:128], q[:, 0:128], start=True, stop=False)
                        pe.matmul(O[:, 0:128], maskb[:, m0, :], identb[:], start=False, stop=True)
                        pe.matmul(O[:, 128:256], kk[:, 0:128], q[:, 128:256], start=True, stop=True)
                        pe.matmul(O[:, 256:384], kk[:, 128:256], q[:, 128:256], start=True, stop=False)
                        ins = pe.matmul(O[:, 256:384], maskb[:, m1, :], identb[:], start=False, stop=True)
                    else:
                        pe.matmul(O[:, 0:256], kk[:, 0:128], q[:, 0:256], start=True, stop=True)
                        ins = pe.matmul(O[:, 256:512], kk[:, 128:256], q[:, 0:256], start=True, stop=True)
                ins.then_inc(scored, 1)

            def values(it, k, g):
                if g == 0:
                    pe.wait_ge(normed, lin(it, k, 1, 1))
                vf = V[:].rearrange("p t h w -> p (t h w)")
                for i in range(2):
                    h = 2 * g + i
                    pe.wait_ge((rest0, rest1)[i], lin(it, k, 4, g + 1))
                    for qt in range(2):
                        o = ps[:, 6 + k % 2, (qt * HU + h) * VW:(qt * HU + h + 1) * VW]
                        kts = [0] if causal and qt == 0 else [0, 1]
                        for kt in kts:
                            off = qt * 128 if kt == 0 else 256 + (0 if causal else qt * 128)
                            at = ((2 * (k // 2) + kt) * H + HU * (k % 2) + h) * VW
                            v = vf[:, bass.ds(it * (4 * H * VW) + at, VW)]
                            pe.matmul(o, probhi[:, g % 2, i, off:off + 128], v, start=(kt == 0), stop=False)
                            ins = pe.matmul(o, problo[:, g % 2, i, off:off + 128], v, start=False,
                                            stop=(kt == kts[-1]))
                ins.then_inc(weighted, 1)

            def slot(it, k):
                v = (k + 2) % 4
                for g in range(4):
                    if g == 0:
                        pe.wait_ge(maxin, lin(it, k, 16, 16))
                    scores(it, k, g)
                    if g == 0 and maxima_left(it, k):
                        max_rows(4 + (k + 1) % 2, lin(it, k, 9, 17), lin(it, k, 1, 2))
                    if heads_left(it, k):
                        if g == 0:
                            pe.wait_ge(loaded[v], lin(it, 0, 8, 32 if k < 2 else 64))
                        for i in range(2):
                            j = 1 + 2 * g + i
                            head_rows(v, 2 * g + i, 4 + (k + 1 + j) % 2, lin(it, k, 9, 17 + j))
                    if g > 0:
                        values(it, k, g - 1)
                values(it, k, 3)

            pe.wait_ge(loaded[0], 32)
            for h in range(HU):
                head_rows(0, h, 4 + h % 2, h)
            pe.wait_ge(loaded[1], 32)
            max_rows(4, 8, 1)
            for h in range(HU):
                head_rows(1, h, 4 + (9 + h) % 2, 9 + h)
            slots(pe, slot)

        @block.scalar
        def _(act):
            act.sem_inc(exped, 2)

            def slot(it, k):
                for g in range(4):
                    act.wait_ge(weighted, lin(it, k, 4, g + 1))
                    act.wait_ge(scored, lin(it, k, 4, g + 1))
                    act.activation(prob[:, g % 2, :, 0:W1], ps[:, 2 * (g % 2):2 * (g % 2) + 2, 0:W1],
                                   ACT.Exp).then_inc(exped, 1)
            slots(act, slot)

        @block.vector
        def _(dve):
            dve.sem_inc(rows_read, 2)
            dve.sem_inc(normed, 2)

            def read_head(h, bank, item):
                dve.wait_ge(rows_done, item + 1)
                dve.tensor_reduce(bmax[:, h, 0:NB], ps[:, bank, 0:NB * BW].rearrange("p (n w) -> p n w", n=NB),
                                  AX.X, ALU.max).then_inc(rows_read, 1)

            def read_max_rows(par, bank, item, written):
                dve.wait_ge(maxout, written)
                dve.wait_ge(rows_done, item + 1)
                dve.tensor_copy(nmT[:, par, :], ps[0:24, bank, :].bitcast(BF16)[:, 0:S]).then_inc(rows_read, 1)

            def split_maxima():
                dve.drain()
                if causal:
                    dve.tensor_tensor(bmax[:, :, 1], bmax[:, :, 1], bmax[:, :, 2], ALU.max)
                    dve.drain()
                dve.tensor_scalar(nmax[:, 0, :, :].rearrange("p q h -> p h q"), bmax[:, :, 0:2], -1.0, None, ALU.mult)
                dve.drain()
                dve.tensor_copy(nparts[:, :, 0, :], nmax[:, 0, :, :])
                dve.drain()
                dve.tensor_tensor(nmax[:, 1, :, :], nmax[:, 0, :, :], nparts[:, :, 0, :], ALU.subtract)
                dve.drain()
                dve.tensor_copy(nparts[:, :, 1, :], nmax[:, 1, :, :])
                dve.drain()
                dve.tensor_tensor(nparts[:, :, 2, :], nmax[:, 1, :, :], nparts[:, :, 1, :],
                                  ALU.subtract).then_inc(maxparts, 1)

            def normalise(it, k):
                dve.drain()
                dve.wait_ge(weighted, lin(it, k, 4, 6))
                o = ps[:, 6 + k % 2, 0:2 * HU * VW].rearrange("p (n w) -> p n w", w=VW)
                dve.reciprocal(rsum[:], o[:, :, 3 * DH])
                dve.tensor_reduce(osum[:], o[:, :, 0:3 * DH].rearrange("p n (a d) -> p n d a", a=3), AX.X,
                                  ALU.add).then_inc(normed, 1)
                dve.drain()
                dst = ao[:, bass.ds(it * (4 * D) + (k // 2) * 2 * D, 2 * D)].rearrange("p (q x) -> p q x", q=2)
                dst = dst[:, :, 64 * (k % 2):64 * (k % 2) + 64].rearrange("p q (h d) -> p q h d", h=HU)
                dve.tensor_tensor(dst, osum[:].rearrange("p (q h) d -> p q h d", q=2),
                                  bc(rsum[:].rearrange("p (q h o) -> p q h o", q=2, o=1), [P, 2, HU, DH]), ALU.mult)

            def slot(it, k):
                if maxima_left(it, k):
                    read_max_rows((k + 1) % 2, 4 + (k + 1) % 2, lin(it, k, 9, 17), lin(it, k, 16, 32))
                for g in range(4):
                    if heads_left(it, k):
                        for j in (2 * g + 1, 2 * g + 2):
                            read_head(j - 1, 4 + (k + 1 + j) % 2, lin(it, k, 9, 17 + j))
                    rest(dve, it, k, g, 0)
                if heads_left(it, k):
                    split_maxima()
                normalise(it, k)

            for h in range(HU):
                read_head(h, 4 + h % 2, h)
            split_maxima()
            read_max_rows(0, 4, 8, 16)
            for h in range(HU):
                read_head(h, 4 + (9 + h) % 2, 9 + h)
            split_maxima()
            slots(dve, slot)

        @block.sync
        def _(sp):
            sp.sem_inc(maxout, 32)

            def load(slot, batch, half):
                for dst, src, n in ((Qs, scrQ, RT), (Ks, scrK, RB)):
                    sp.dma_start(dst[0:n, slot, :, :],
                                 src[:, half * HU:half * HU + HU, bass.ds(batch, S)]).then_inc(loaded[slot], 16)

            def maxima(par, slot, item, before, after):
                wait_apart(sp, rows_read, item + 3, passed)
                sp.wait_ge(maxin, before)
                sp.dma_start(scrM[par], nmT[:, par, :]).then_inc(maxout, 16)
                sp.wait_ge(maxout, after)
                sp.dma_start(Qs[RB:RM, slot, :, :],
                             scrM[par].rearrange("(a h) q -> a h q", a=3)).then_inc(maxin, 16)

            for u in range(4):
                load(u, (u // 2) * S, u % 2)
            if a < 4:
                total = load_experts(nc, st, sp, st["wsem"][a], a, dr) if a > 0 else 0
            sp.wait_ge(rows_read, 8 + 3)
            sp.dma_start(scrM[0], nmT[:, 0, :]).then_inc(maxout, 16)
            sp.wait_ge(maxout, 48)
            sp.dma_start(Qs[RB:RM, 0, :, :], scrM[0].rearrange("(a h) q -> a h q", a=3)).then_inc(maxin, 16)

            def slot(it, k):
                if maxima_left(it, k):
                    item, before, after = (lin(it, k, 9, 17), lin(it, k, 16, 16), lin(it, k, 16, 64))
                    maxima((k + 1) % 2, (k + 1) % 4, item, before, after)
                if not isinstance(it, int):
                    at = sp.snap(it * (2 * S) + (k // 2 + 2) * S)
                    wait_apart(sp, scored, lin(it, k, 4, 4), passed)
                    load(k, at, k % 2)
            slots(sp, slot)


def output_stage(nc, st, sem, a):
    ended = sem.next_stage()
    own = a == 4
    ps, x, xnT, ao, kf, rows, cols = (st[k] for k in ("ps", "x", "xnT", "ao", "kf", "rows", "cols"))
    wo = st["wp"][:, W_OFF["o", a]:W_OFF["o", a] + D]
    s_t, s_c, s_o, s_r, s_x = (sem(f"o{a}_{k}") for k in ("transposed", "copied", "projected", "read", "added"))
    with nc.Block() as block:
        @block.gpsimd
        def _(pool):
            pool.sem_clear(ended)

        @block.tensor
        def _(pe):
            def turn(c):
                for k in range(4):
                    t = 4 * c + k
                    ins = pe.transpose(ps[:, c, k * P:(k + 1) * P], ao[:, t * D:(t + 1) * D], st["ident"][:])
                ins.then_inc(s_t, 1)
            turn(0)
            for c in range(NC):
                if c + 1 < NC:
                    turn(c + 1)
                pe.wait_ge(s_c, c + 1)
                if own:
                    ins = pe.matmul(ps[:, 4 + c, :], wo, kf[:, c % 2, :], start=True, stop=True)
                else:
                    for k in range(4):
                        ins = pe.matmul(ps[:, 4 + c, k * P:(k + 1) * P], kf[:, c % 2, k * P:(k + 1) * P], wo,
                                        start=True, stop=True)
                ins.then_inc(s_o, 1)

        @block.scalar
        def _(act):
            for c in range(NC):
                act.wait_ge(s_t, c + 1)
                if c >= 2:
                    act.wait_ge(s_o, c - 1)
                act.copy(kf[:, c % 2, :], ps[:, c, :]).then_inc(s_c, 1)
                if own and c >= 1:
                    act.wait_ge(s_o, c)
                    act.activation(xnT[:, (c - 1) * CH:c * CH], ps[:, 4 + c - 1, :], ACT.Identity,
                                   bias=cols[:, C_OFF["o", 4]:C_OFF["o", 4] + 1])
            if own:
                act.wait_ge(s_o, NC)
                act.activation(xnT[:, 3 * CH:], ps[:, 7, :], ACT.Identity,
                               bias=cols[:, C_OFF["o", 4]:C_OFF["o", 4] + 1])

        if not own:
            @block.vector
            def _(dve):
                bo = rows[:, R_OFF["o", a]:R_OFF["o", a] + D]
                for c in range(NC):
                    dve.wait_ge(s_o, c + 1)
                    xc = x[:, c * CH:(c + 1) * CH]
                    if a == 0:
                        for k in range(4):
                            t = 4 * c + k
                            dve.scalar_tensor_tensor(ao[:, t * D:(t + 1) * D], ps[:, 4 + c, k * P:(k + 1) * P],
                                                     st["qkeep"][:, t:t + 1], bo, ALU.mult, ALU.add)
                    else:
                        dve.tensor_tensor(ao[:, c * CH:(c + 1) * CH].rearrange("p (t d) -> p t d", t=4),
                                          ps[:, 4 + c, :].rearrange("p (t d) -> p t d", t=4),
                                          bc(bo.rearrange("p (o d) -> p o d", o=1), [P, 4, D]), ALU.add)
                    dve.drain()
                    dve.scalar_tensor_tensor(xc, ao[:, c * CH:(c + 1) * CH], st["gate"][:, a:a + 1], xc,
                                             ALU.mult, ALU.add)


def route_stage(nc, st, sem, l, dr):
    ended = sem.next_stage()
    ps, xnT, wp, rows, rt, top, small, coef = (
        st[k] for k in ("ps", "xnT", "wp", "rows", "rt", "top", "small", "coef"))
    E = MOE[l]["E"]
    own = l == 3
    s_var, s_rstd, s_xn, s_xt, s_xc = (sem(f"r{l}_{k}") for k in ("var", "rstd", "xn", "xt", "xc"))
    s_l, s_d, s_a, s_c, s_t = (sem(f"r{l}_{k}") for k in ("logits", "shifted", "exps", "coefs", "turned"))
    lg = ps[:, 0:2, :].rearrange("p b c -> p (b c)")[:, 0:NT * E].rearrange("p (t e) -> p t e", e=E)
    A, Bf, Cf, Df = (rt[:, i, :, 0:E] for i in range(4))

    xh, wf, whi = st["xh"], st["wf"], st["whi"]
    s_xh, s_wh, s_wl, s_wd = (sem(f"r{l}_{k}") for k in ("x_first", "w_first", "w_second", "w_done"))
    wcols = {0: 0, 1: 2 * 33 * P, 2: 28 * P, 3: 16 * P}[l]
    wcuts = [(i, min(i + 1056, wcols)) for i in range(0, wcols, 1056)]
    wparts = wf[:].bitcast(F16).rearrange("p (c two) -> p two c", two=2)

    def wide(v, e=E):
        return bc(v.rearrange("p (t o) -> p t o", o=1), [P, NT, e])

    with nc.Block() as block:
        @block.tensor
        def _(pe):
            if not own:
                norm_tensor(nc, st, pe, s_xn, s_xt, 4)
            for t in range(NT):
                if not own and t % 4 == 0:
                    pe.wait_ge(s_xc, t // 4 + 1)
                ins = pe.matmul(lg[:, t, :], xnT[:, t * P:(t + 1) * P], wp[:, W_OFF["r", l]:W_OFF["r", l] + E],
                                start=True, stop=True)
            ins.then_inc(s_l, 1)
            pe.wait_ge(s_c, 1)
            turned = ps[:, 2:4, :].rearrange("p b c -> p (b c)").bitcast(F16)
            for t in range(NT):
                ins = pe.transpose(turned[0:2 * E, t * P:(t + 1) * P], coef[:, t, 0:2 * E], st["identh"][:])
            ins.then_inc(s_t, 1)

        @block.gpsimd
        def _(pool):
            pool.sem_clear(ended)
            if not own:
                norm_pool(nc, st, pool, s_var, s_rstd)
            if l > 0:
                for c in range(NC):
                    pool.wait_ge(s_xh, c + 1)
                    sl = slice(c * CH, (c + 1) * CH)
                    pool.tensor_tensor(xh[:, 1, sl], xnT[:, sl], xh[:, 0, sl], ALU.subtract)
                for i, (lo, hi) in enumerate(wcuts):
                    pool.wait_ge(s_wh, i + 1)
                    pool.tensor_tensor(wparts[:, 1, lo:hi], wf[:, lo:hi], whi[:, lo:hi], ALU.subtract).then_inc(s_wl, 1)

        @block.scalar
        def _(act):
            if not own:
                norm_scalar(nc, st, act, s_xt, s_xc, 4)
            if l > 0:
                for c in range(NC):
                    if not own:
                        act.wait_ge(s_xc, c + 1)
                    act.copy(xh[:, 0, c * CH:(c + 1) * CH], xnT[:, c * CH:(c + 1) * CH]).then_inc(s_xh, 1)
                act.wait_ge(st["wsem"][l], {1: 48, 2: 32, 3: 32}[l])
                for i in range(len(wcuts)):
                    lo, hi = wcuts[i]
                    act.copy(whi[:, lo:hi], wf[:, lo:hi]).then_inc(s_wh, 1)
                for i in range(len(wcuts)):
                    lo, hi = wcuts[i]
                    act.wait_ge(s_wl, i + 1)
                    act.copy(wparts[:, 0, lo:hi], whi[:, lo:hi]).then_inc(s_wd, 1)
            if l == 1:
                act.wait_ge(s_l, 1)
                act.wait_ge(s_wd, len(wcuts))
                act.activation(A, lg, ACT.Sigmoid).then_inc(s_a, 1)
            else:
                act.wait_ge(s_d, 1)
                act.activation(Bf, Bf, ACT.Exp).then_inc(s_a, 1)
            act.wait_ge(s_t, 1)
            turned = ps[:, 2:4, :].rearrange("p b c -> p (b c)").bitcast(F16)
            act.copy(st["coefT"][0:2 * E, :], turned[0:2 * E, :])

        @block.vector
        def _(dve):
            if not own:
                norm_vector(nc, st, dve, s_var, s_rstd, s_xn)
            dve.wait_ge(s_l, 1)
            if l > 0:
                dve.wait_ge(s_wd, len(wcuts))
            if l == 1:
                G = 8
                eb = bc(rows[:, R_OFF["ebias"]:R_OFF["ebias"] + E].rearrange("p (o e) -> p o e", o=1), [P, NT, E])
                dve.wait_ge(s_a, 1)
                dve.tensor_tensor(Bf, A, eb, ALU.add)
                dve.drain()
                g4 = [v.rearrange("p t (g e) -> p (t g) e", g=G) for v in (A, Bf, Cf, Df)]
                m1, m2, cnt, gs = (small[:, i, :, :] for i in range(4))
                m1f, m2f, cntf = (v.rearrange("p t (g o) -> p (t g) o", o=1) for v in (m1, m2, cnt))
                dve.tensor_reduce(m1f, g4[1], AX.X, ALU.max)
                dve.drain()
                dve.tensor_tensor(g4[2], g4[1], bc(m1f, [P, NT * G, 8]), ALU.is_equal)
                dve.drain()
                dve.tensor_reduce(cntf, g4[2], AX.X, ALU.add)
                dve.scalar_tensor_tensor(Df.rearrange("p t e -> p (t e)"), Cf.rearrange("p t e -> p (t e)"), -BIG,
                                         Bf.rearrange("p t e -> p (t e)"), ALU.mult, ALU.add)
                dve.drain()
                dve.tensor_reduce(m2f, g4[3], AX.X, ALU.max)
                dve.tensor_scalar(cnt, cnt, 1.5, None, ALU.is_ge)
                dve.drain()
                dve.tensor_tensor(gs, cnt, m1, ALU.mult)
                dve.tensor_scalar(cnt, cnt, 1.0, BIG, ALU.subtract, ALU.mult)
                dve.drain()
                dve.tensor_tensor(gs, gs, cnt, ALU.add)
                dve.drain()
                dve.tensor_tensor(gs, gs, m2, ALU.max)
                dve.drain()
                dve.tensor_tensor(gs, gs, m1, ALU.add)
                dve.drain()
                for t in range(NT):
                    dve.max(top[:, t, :], gs[:, t, :])
                dve.drain()
                dve.tensor_tensor(gs, gs, wide(top[:, :, 3], G), ALU.is_ge)
                dve.drain()
                dve.tensor_tensor(g4[2], g4[1], bc(gs.rearrange("p t (g o) -> p (t g) o", o=1), [P, NT * G, 8]),
                                  ALU.mult)
                dve.drain()
                for t in range(NT):
                    dve.max(top[:, t, :], Cf[:, t, :])
                dve.drain()
                for t in range(NT):
                    dve.match_replace(Df[:, t, :], top[:, t, :], Cf[:, t, :], -BIG)
                dve.drain()
                dve.tensor_scalar(Df, Df, -BIG / 2, None, ALU.is_le)
                dve.drain()
                dve.tensor_tensor(Bf, A, Df, ALU.mult)
                scale, tiny = 2.5, 1e-20
            else:
                if l == 2:
                    dve.tensor_copy(A, lg)
                else:
                    rb = rows[:, R_OFF["r", l]:R_OFF["r", l] + E].rearrange("p (o e) -> p o e", o=1)
                    dve.tensor_tensor(A, lg, bc(rb, [P, NT, E]), ALU.add)
                dve.drain()
                for t in range(NT):
                    dve.max(top[:, t, :], A[:, t, :])
                dve.drain()
                dve.tensor_tensor(Bf, A, wide(top[:, :, 0]), ALU.subtract).then_inc(s_d, 1)
                dve.tensor_tensor(Cf, A, wide(top[:, :, 0 if l == 2 else 1]), ALU.is_ge)
                dve.drain()
                dve.wait_ge(s_a, 1)
                scale, tiny = {0: (2.0, None), 2: (1.0, None), 3: (0.3, 1e-8)}[l]
                s0 = small[:, 0, :, 0]
                if l != 0:
                    dve.tensor_reduce(s0, Bf, AX.X, ALU.add)
                    dve.drain()
                    dve.reciprocal(s0, s0)
                    dve.drain()
                    dve.tensor_tensor(Bf, Bf, wide(s0), ALU.mult)
                    dve.drain()
                dve.tensor_tensor(Bf, Bf, Cf, ALU.mult)
            dve.drain()
            if l != 2:
                s1 = small[:, 1, :, 0]
                dve.tensor_reduce(s1, Bf, AX.X, ALU.add)
                dve.drain()
                if tiny:
                    dve.tensor_scalar(s1, s1, tiny, None, ALU.add)
                    dve.drain()
                dve.reciprocal(s1, s1)
                dve.drain()
                dve.tensor_scalar(s1, s1, scale, None, ALU.mult)
                dve.drain()
                dve.tensor_tensor(Bf, Bf, wide(s1), ALU.mult)
                dve.drain()
            dve.tensor_copy(coef[:, :, 0:E], Bf)
            dve.drain()
            dve.tensor_tensor(coef[:, :, E:2 * E], Bf, coef[:, :, 0:E], ALU.subtract).then_inc(s_c, 1)



def expert_stage(nc, st, sem, l):
    ended = sem.next_stage()
    ps, x, xn, xnT, xh, wp, wf, cols, hid, sel, coefT, b2h = (
        st[k] for k in ("ps", "x", "xn", "xnT", "xh", "wp", "wf", "cols", "hid", "sel", "coefT", "b2h"))
    J, E, f = MOE[l]["J"], MOE[l]["E"], MOE[l]["f"]
    gated = l == 1
    N = J + gated
    lead = 0 if N == 1 else 2 if N % 2 else 1
    pairs = (N - 1 - lead) // 2
    up, acted, weighed, down, added = (
        sem(f"e{l}_{k}") for k in ("up", "activated", "weighed", "down", "added"))
    loaded, loaded_to = st["wsem"][l], {0: 0, 1: 48, 2: 32, 3: 32}[l]
    GB, UB, CB, YB = 0, 2, 4, 6
    g = st["gate"][:, 4 + l:5 + l]

    def weights(which, j):
        if l == 0:
            o = W_OFF[("loraA", None, "loraB")[which]]
            return wp[:, o:o + D]
        return wf[:, bass.ds(j * P + (which if gated else which // 2) * N * P, P)]

    def weight_parts(which, part, j):
        w = wf[:].bitcast(F16).rearrange("p (c two) -> p two c", two=2)
        return w[:, part, bass.ds(j * P + which * N * P, P)]

    def selector(j, half_j):
        o = SEL_OFF[l]
        if l < 2:
            return sel[0:2 * E, bass.ds(j * P + (o - gated * P), P)]
        return sel[0:2 * E, bass.ds(half_j * P + o, P)]

    def steps(eng, c, body):
        for s in range(lead):
            body(s, s, s + 1, (s + 1) // 2)
        if pairs:
            with eng.Fori(0, pairs) as p:
                for k in range(2):
                    s0 = lead + k
                    body(p * 2 + s0, s0, p * 2 + (s0 + 1), p + (s0 + 1) // 2)

    with nc.Block() as block:
        @block.gpsimd
        def _(pool):
            pool.sem_clear(ended)

        @block.tensor
        def _(pe):
            pe.sem_inc(down, 2)
            if loaded_to:
                pe.wait_ge(loaded, loaded_to)

            def product(out, which, j, c):
                if l == 0:
                    return pe.matmul(out, weights(which, j), xnT[:, c * CH:(c + 1) * CH], start=True, stop=True)
                for i, (wpart, xpart) in enumerate(((0, 0), (0, 1), (1, 0))):
                    ins = pe.matmul(out, weight_parts(which, wpart, j), xh[:, xpart, c * CH:(c + 1) * CH],
                                    start=(i == 0), stop=(i == 2))
                return ins

            def do_up(c, j, par, half_j):
                m, r = N * c, (N * c + par) % 2
                shared = gated and isinstance(j, int) and j == 0
                pe.wait_ge(weighed, j + (m + 1))
                if gated:
                    product(ps[:, UB + r, :], 1, j, c)
                ins = product(ps[:, GB + r, :], 0, j, c)
                if not shared:
                    ins = pe.matmul(ps[:, CB + r, :], selector(j, half_j), coefT[0:2 * E, c * CH:(c + 1) * CH],
                                    start=True, stop=True)
                ins.then_inc(up, 1)

            def do_down(c, j, par, first, last):
                pe.wait_ge(weighed, j + (N * c + 3))
                for k in range(4):
                    ins = pe.matmul(ps[:, YB + c % 2, k * P:(k + 1) * P],
                                    hid[:, (N * c + par) % 2, 1, k * P:(k + 1) * P], weights(2, j),
                                    start=(first and k == 0), stop=last, skip_group_check=True)
                ins.then_inc(down, 1)

            for c in range(NC):
                do_up(c, 0, 0, 0)
                if c >= 2:
                    pe.wait_ge(added, c - 1)
                for k in range(4):
                    tok = slice(c * CH + k * P, c * CH + (k + 1) * P)
                    y = ps[:, YB + c % 2, k * P:(k + 1) * P]
                    if l == 0:
                        pe.matmul(y, xnT[:, tok], wp[:, W_OFF["base"]:W_OFF["base"] + D], start=(k == 0), stop=False,
                                  skip_group_check=True)
                    elif l > 1:
                        for part in range(2):
                            pe.matmul(y, coefT[0:2 * E, tok], b2h[0:2 * E, part, l - 2, :],
                                      start=(part == 0 and k == 0), stop=False, skip_group_check=True)

                def step(s, par, s1, half):
                    do_up(c, s1, par + 1, half)
                    do_down(c, s, par, gated and isinstance(s, int) and s == 0, False)
                steps(pe, c, step)
                do_down(c, N - 1, N - 1, False, True)

        @block.scalar
        def _(act):
            def do_act(c, j, par):
                r = (N * c + par) % 2
                act.wait_ge(weighed, j + (N * c + 1))
                act.wait_ge(up, j + (N * c + 1))
                bias = 0.0 if l < 2 else cols[:, bass.ds(j + C_OFF["b1", l], 1)]
                act.activation(hid[:, r, 0, :], ps[:, GB + r, :], f, bias=bias).then_inc(acted, 1)

            for c in range(NC):
                do_act(c, 0, 0)
                steps(act, c, lambda s, par, s1, half: do_act(c, s1, par + 1))

        @block.vector
        def _(dve):
            dve.sem_inc(weighed, 2)
            if l == 3:
                dve.scalar_tensor_tensor(x[:], xn[:], g, x[:], ALU.mult, ALU.add)
            if l == 0:
                x3 = x[:].rearrange("p (t d) -> p t d", d=D)
                base = st["rows"][:, R_OFF["base"]:R_OFF["base"] + D].rearrange("p (o d) -> p o d", o=1)
                dve.scalar_tensor_tensor(x3, bc(base, [P, NT, D]), g, x3, ALU.mult, ALU.add)

            def weigh(c, j, par):
                r = (N * c + par) % 2
                shared = gated and isinstance(j, int) and j == 0
                dve.wait_ge(acted, j + (N * c + 1))
                dve.wait_ge(down, j + (N * c + 1))
                h0, h1 = hid[:, r, 0, :], hid[:, r, 1, :]
                if shared:
                    dve.tensor_tensor(h1, h0, ps[:, UB + r, :], ALU.mult).then_inc(weighed, 1)
                    return
                if gated:
                    dve.tensor_tensor(h0, h0, ps[:, UB + r, :], ALU.mult)
                    dve.drain()
                dve.tensor_tensor(h1, h0, ps[:, CB + r, :], ALU.mult).then_inc(weighed, 1)

            def add(c):
                dve.wait_ge(down, N * (c + 1) + 2)
                xc = x[:, c * CH:(c + 1) * CH]
                dve.scalar_tensor_tensor(xc, ps[:, YB + c % 2, :], g, xc, ALU.mult, ALU.add).then_inc(added, 1)

            for c in range(NC):
                weigh(c, 0, 0)
                if c > 0:
                    add(c - 1)
                steps(dve, c, lambda s, par, s1, half: weigh(c, s1, par + 1))
            add(NC - 1)


_OUT = (B, S, D)


def kernel(**inputs):
    import numpy as np
    import concourse.bacc as bacc
    from concourse.bass_utils import run_bass_kernel_spmd

    a = {k: np.asarray(v) for k, v in inputs.items()}

    def dims_major(w):
        return w.reshape(w.shape[0], H, DH).transpose(0, 2, 1).reshape(w.shape[0], H * DH)

    def pad_heads(w):
        return np.concatenate([w.reshape(w.shape[0], H, 4), np.zeros((w.shape[0], H, 4), np.float32)],
                              axis=2).reshape(w.shape[0], H * DH)

    xa = [{k: a[f"L{l}_xattn_{n}"].T for k, n in zip("qkvo", ("Wq", "Wk", "Wv", "Wo"))} for l in (0, 1, 3)]
    xa.insert(2, {k: a[f"L2_xattn_w_{k}"].T for k in "qkvo"})
    xa.append({"q": a["L3_ffn_q_w"], "k": pad_heads(a["L3_ffn_k_w"]), "v": pad_heads(a["L3_ffn_v_w"]),
               "o": pad_heads(a["L3_ffn_o_w"][0:64].T).T})
    zero = np.zeros((1, D), np.float32)
    bias = [{k: a[f"L0_xattn_b{k}"][None] for k in "qkvo"},
            {"q": zero, "k": zero, "v": a["L1_xattn_bv"][None], "o": a["L1_xattn_bo"][None]},
            {k: zero for k in "qkvo"},
            {k: a[f"L3_xattn_b{k}"][None] for k in "qkvo"},
            {"q": a["L3_ffn_q_b"][None], "k": pad_heads(a["L3_ffn_k_b"][None]),
             "v": pad_heads(a["L3_ffn_v_b"][None]), "o": a["L3_ffn_o_b"][None]}]
    w = []
    for m in xa:
        w += [dims_major(m["q"]), dims_major(m["k"]), m["v"], m["o"]]
    w += [a["L0_ffn_base_w"].T, a["L0_ffn_lora_A"].transpose(1, 0, 2).reshape(D, P),
          a["L0_ffn_lora_B"].reshape(P, D)]
    w += [a["L0_ffn_router_w"].T, a["L1_ffn_router_w"].T, a["L2_ffn_router_w"], a["L3_ffn_router_w"]]
    cols = []
    for m in bias:
        cols += [dims_major(m["q"]), dims_major(m["k"])]
    cols += [a["L0_ffn_base_b"][None], a["L2_ffn_b1"].reshape(28, P), a["L3_ffn_b1"].reshape(16, P), zero]

    def constant_rows(parts):
        out = np.zeros((1, D), np.float32)
        for i, p in enumerate(parts):
            out[0, 16 * i:16 * i + 16] = p
        return out

    cols += [constant_rows([BIG]), constant_rows([998244352.0, 1753088.0, 2560.0]), a["L3_ffn_o_b"][None]]
    rows = []
    for m in bias:
        rows += [m["v"], m["o"]]
    rows += [a["L0_ffn_base_b"][None], a["L0_ffn_router_b"][None], a["L3_ffn_router_b"][None], a["L1_ffn_e_bias"][None],
             a["g_xattn"][None], a["g_ffn"][None]]
    sel = np.zeros((P, SEL_N), np.float16)
    for l in range(4):
        E = MOE[l]["E"]
        n = {0: 1, 1: 32, 2: 14, 3: 8}[l]
        for i in range(n):
            for j in range(P):
                e = {0: j // 16, 1: 2 * i + j // 64}.get(l, i)
                sel[[e, e + E], SEL_OFF[l] + i * P + j] = 1
    low = np.tril(np.ones((P, P), np.float32))
    strict = np.tril(np.ones((P, P), np.float32), -1)
    strict0 = strict.copy()
    strict0[0, 0] = 1
    causal = np.stack([np.where(m > 0, 0.0, -BIG).astype(np.float32) for m in (low, strict, strict0)], axis=1)

    def pairs_of(g, s):
        return np.concatenate([s, g.transpose(1, 0, 2).reshape(D, 64 * 64)], axis=1)

    def down(w2):
        return w2.transpose(1, 0, 2).reshape(P, -1)

    b2 = np.zeros((2, 28, D), np.float32)
    b2[0, 0:14] = b2[0, 14:28] = a["L2_ffn_b2"]
    b2[1, 0:8] = b2[1, 8:16] = a["L3_ffn_b2"]
    arrays = {
        "x": a["x"], "ctx": a["ctx_1024"], "mask": a["mask_BxS2_ik0"],
        "wpack": np.concatenate(w, axis=1), "cols": np.concatenate(cols, axis=0).T, "rows": np.concatenate(rows, axis=1)[0],
        "b2": b2, "ident": np.eye(P, dtype=np.float32), "causal": causal, "sel": sel,
        "L1_wg": pairs_of(a["L1_ffn_Wg"], a["L1_ffn_SWg"]), "L1_wu": pairs_of(a["L1_ffn_Wu"], a["L1_ffn_SWu"]),
        "L1_wd": np.concatenate([a["L1_ffn_SWd"], down(a["L1_ffn_Wd"].reshape(32, P, D))], axis=1),
        "L2_w1": a["L2_ffn_w1"].transpose(1, 0, 2).reshape(D, 14 * 256),
        "L2_w2": down(a["L2_ffn_w2"].reshape(28, P, D)),
        "L3_w1": a["L3_ffn_w1"].transpose(1, 0, 2).reshape(D, 8 * 256),
        "L3_w2": down(a["L3_ffn_w2"].reshape(16, P, D)),
    }
    arrays = {k: np.ascontiguousarray(v) for k, v in arrays.items()}
    nc = bacc.Bacc("TRN2", target_bir_lowering=False, num_devices=1)
    dr = {k: nc.dram_tensor(f"in_{k}", v.shape, mybir.dt.from_np(v.dtype), kind="ExternalInput").ap()
          for k, v in arrays.items()}
    out = nc.dram_tensor("out", _OUT, F32, kind="ExternalOutput").ap()
    build(nc, dr, out)
    r = run_bass_kernel_spmd(nc, [{f"in_{k}": v for k, v in arrays.items()}], core_ids=[0])
    return r.results[0]["out"]
```

```python
from contextlib import ExitStack

import concourse.bass as bass
from concourse import mybir

F32 = mybir.dt.float32
F16 = mybir.dt.float16
BF16 = mybir.dt.bfloat16
I32 = mybir.dt.int32
ACT = mybir.ActivationFunctionType
ALU = mybir.AluOpType
AX = mybir.AxisListType

P = 128
B, S, D = 8, 256, 128
T = B * S
NT = T // P
CH = 512
NC = T // CH
H, DH = 16, 8
EPS = 1e-5
HU = 8
NU = B * H // HU
RT = 6 * DH
RB = RT + 3
RM = RB + 3
WARM = 20
BIG = float(2.0 ** 100)
Q_PARTS = (0, 0, 0, 1, 2, 1)
K_PARTS = (1, 2, 0, 0, 0, 1)
VW = 3 * DH + 1

ATT = [
    dict(causal="incl", keymask=True, dk=8, dv=8, gate=0),
    dict(causal="strict", keymask=False, dk=8, dv=8, gate=1),
    dict(causal=None, keymask=True, dk=8, dv=8, gate=2),
    dict(causal="incl", keymask=False, dk=8, dv=8, gate=3),
    dict(causal=None, keymask=False, dk=4, dv=4, gate=None),
]
MOE = [
    dict(E=8, J=1, f=ACT.Identity),
    dict(E=64, J=32, f=ACT.Silu),
    dict(E=14, J=28, f=ACT.Gelu),
    dict(E=8, J=16, f=ACT.Gelu),
]
for _l, _m in enumerate(MOE):
    _m["blocks"] = _m["J"] + (_l == 1)
    _m["mats"] = 0 if _l == 0 else 3 if _l == 1 else 2
    _m["cols"] = _m["blocks"] * P
W_OFF, n = {}, 0
for _l in range(5):
    for _k in "qkvo":
        W_OFF[_k, _l] = n
        n += D
for _k in ("base", "loraA", "loraB"):
    W_OFF[_k] = n
    n += D
for _l in range(4):
    W_OFF["r", _l] = n
    n += MOE[_l]["E"]
W_N = n
C_OFF, n = {}, 0
for _l in range(5):
    for _k in "qk":
        C_OFF[_k, _l] = n
        n += 1
C_OFF["base"] = n
C_OFF["b1", 2] = n + 1
C_OFF["b1", 3] = n + 1 + 28
C_OFF["zero"] = n + 1 + 28 + 16
C_OFF["o", 4] = C_OFF["zero"] + 3
C_OFF["cmask", 0] = C_OFF["zero"] + 1
C_OFF["cmask", 2] = C_OFF["zero"] + 2
C_N = C_OFF["zero"] + 4
R_OFF, n = {}, 0
for _l in range(5):
    for _k in "vo":
        R_OFF[_k, _l] = n
        n += D
for _k, _w in (("base", D), (("r", 0), 8), (("r", 3), 8), ("ebias", 64), ("g", 8)):
    R_OFF[_k] = n
    n += _w
R_N = n
SEL_OFF = {0: 0, 1: 128, 2: 128 + 32 * 128, 3: 128 + 32 * 128 + 14 * 128}
SEL_N = 128 * (1 + 32 + 14 + 8)
WF = 3 * 33 * 128


def build(nc, dr, out):
    with ExitStack() as ctx:
        def sb(name, shape, dt=F32):
            return ctx.enter_context(nc.sbuf_tensor(name, shape, dt))

        def sem(name):
            return ctx.enter_context(nc.semaphore(name))

        ps = ctx.enter_context(nc.psum_tensor("ps", [P, 8, CH], F32))
        x = sb("x", [P, NT * D])
        xn = sb("xn", [P, NT * D])
        xnT = sb("xnT", [P, T])
        ctxT = sb("ctxT", [P, T])
        ao = sb("ao", [P, NT * D])
        xh = ao[:].bitcast(F16).rearrange("p (a t) -> p a t", a=2)
        wp = sb("wp", [P, W_N])
        wf = sb("wf", [P, WF])
        cols = sb("cols", [P, C_N])
        rows = sb("rows", [P, R_N])
        b2 = sb("b2", [28, 2, D])
        b2h = sb("b2h", [28, 2, 2, D], F16)
        ident = sb("ident", [P, P])
        identb = sb("identb", [P, P], BF16)
        identh = sb("identh", [P, P], F16)
        maskb = sb("maskb", [P, 3, P], BF16)
        maskf = sb("maskf", [P, 3, P])
        sel = sb("sel", [P, SEL_N], F16)
        keep = sb("keep", [P, T], BF16)
        qkeep = sb("qkeep", [P, NT])
        minus = sb("minus", [P, 1, 1])
        gate = sb("gate", [P, 8])
        V = sb("V", [P, NT, H, VW], BF16)
        stats = sb("stats", [P, NT, 6])
        mom = sb("mom", [P, 6, NT])
        rstd = sb("rstd", [P, NT])
        neghalf = sb("neghalf", [P, NT])
        qb = sb("qb", [P, 5])
        top = sb("top", [P, NT, 8])
        small = sb("small", [P, 4, NT, 8])
        coefT = sb("coefT", [P, T], F16)
        Qs = sb("Qs", [RM, 4, HU, S], BF16)
        Ks = sb("Ks", [RM, 4, HU, S], BF16)
        work = sb("work", [P, 5248])
        kf = work[:, 0:1024].rearrange("p (k c) -> p k c", k=2)
        rem = ao[:].rearrange("p (k c) -> p k c", k=4)
        parts = work[:, 1024:4096].bitcast(BF16).rearrange("p (k a c) -> p k a c", k=4, a=3)
        vf = work[:, 4096:5120].rearrange("p (k c) -> p k c", k=2)
        biasrow = coefT[0:48, :].bitcast(BF16)
        prob = work[:, 0:2048].rearrange("p (r i c) -> p r i c", r=2, i=2)
        probhi = work[:, 0:2048].bitcast(BF16).rearrange("p (r i c two) -> p r i two c", r=2, i=2, two=2)[:, :, :, 1]
        problo = work[:, 2048:3072].bitcast(F16).rearrange("p (r i c) -> p r i c", r=2, i=2)
        rt = work[:, 0:4096].rearrange("p (r t e) -> p r t e", r=4, t=NT)
        coef = work[:, 4224:5248].bitcast(F16).rearrange("p (t e) -> p t e", t=NT)
        hid = work[:, 0:2048].rearrange("p (r k c) -> p r k c", r=2, k=2)
        hparts = work[:, 2048:4096].bitcast(F16).rearrange("p (r k c) -> p r k c", r=4, k=2)
        yT = work[:, 4096:4608]
        whi = work[:, 3072:5248].bitcast(F16)
        bmax = sb("bmax", [P, 2, HU, 3])
        nmax = sb("nmax", [P, 2, 2, HU])
        nparts = sb("nparts", [P, 2, 3, HU], BF16)
        nmT = sb("nmT", [24, 2, S], BF16)
        rsum = sb("rsum", [P, 2, 2 * HU])
        osum = sb("osum", [P, 2, 2 * HU, DH])

        scrQ = nc.dram_tensor("scrQ", [RT, H, T], BF16, kind="Internal").ap()
        scrK = nc.dram_tensor("scrK", [RB, H, T], BF16, kind="Internal").ap()
        scrM = nc.dram_tensor("scrM", [2, 24, S], BF16, kind="Internal").ap()

        wsem = [sem(f"experts_loaded{l}") for l in range(4)]
        s_out = sem("s_out")
        st = dict(locals())
        sem = StageSemaphores(nc)
        setup_stage(nc, st, dr, sem)
        for l in range(4):
            project_stage(nc, st, sem, l, dr)
            attend_stage(nc, st, sem, l, dr)
            output_stage(nc, st, sem, l)
            if l == 3:
                norm_stage(nc, st, sem, "n3")
                project_stage(nc, st, sem, 4, dr)
                attend_stage(nc, st, sem, 4, dr)
                output_stage(nc, st, sem, 4)
            route_stage(nc, st, sem, l, dr)
            if l == 0:
                adapter_stage(nc, st, sem)
            else:
                expert_stage(nc, st, sem, l)
        with nc.Block() as block:
            @block.sync
            def _(sp):
                sp.dma_start(out.rearrange("b (t p) d -> p (b t) d", p=P),
                             x[:].rearrange("p (t d) -> p t d", d=D)).then_inc(s_out, 16)
                sp.wait_ge(s_out, 16)


class StageSemaphores:
    COUNT = 32

    def __init__(self, nc):
        free = sorted(nc.free_semaphores)
        self.nc, self.turn, self.open, self.used = nc, 0, [], 0
        self.first = []
        for n in free:
            if all(n + i in free for i in range(2 * self.COUNT)):
                self.first = [n, n + self.COUNT]
                break

    def next_stage(self):
        for s in self.open:
            self.nc.release_semaphore(s)
        last = range(self.first[self.turn], self.first[self.turn] + self.COUNT)
        self.open, self.used, self.turn = [], 0, 1 - self.turn
        return last

    def __call__(self, name):
        assert self.used < self.COUNT
        s = self.nc.alloc_semaphore(name=name, num=self.first[self.turn] + self.used)
        self.used += 1
        self.open.append(s)
        return s


def wait_apart(sp, semaphore, value, passed):
    sp.wait_ge(semaphore, value)
    sp.sem_inc(passed, 1)


def bc(ap, shape):
    return ap.to_broadcast(shape)


def setup_stage(nc, st, dr, sem):
    ps, x, wp, cols, rows, b2 = (st[k] for k in ("ps", "x", "wp", "cols", "rows", "b2"))
    ao, ctxT, ident = st["ao"], st["ctxT"], st["ident"]
    maski = st["xnT"][:].bitcast(I32)
    qmaski = st["stats"][:].rearrange("p a b -> p (a b)").bitcast(I32)[:, 0:NT]
    s_in = sem("set_loaded")
    s_ctx = sem("set_ctx_loaded")
    s_t = sem("set_transposed")
    with nc.Block() as block:
        @block.sync
        def _(sp):
            sp.dma_start(ao[:].rearrange("p (t d) -> p t d", d=D),
                         dr["ctx"].rearrange("b (t p) d -> p (b t) d", p=P)).then_inc(s_ctx, 16)
            sp.dma_start(ident[:], dr["ident"]).then_inc(s_ctx, 16)
            sp.dma_start(x[:].rearrange("p (t d) -> p t d", d=D),
                         dr["x"].rearrange("b (t p) d -> p (b t) d", p=P)).then_inc(s_in, 16)
            sp.dma_start(wp[:], dr["wpack"]).then_inc(s_in, 16)
            sp.dma_start(cols[:], dr["cols"]).then_inc(s_in, 16)
            sp.dma_start(rows[:], dr["rows"].partition_broadcast(P)).then_inc(s_in, 16)
            sp.dma_start(b2[:], dr["b2"].rearrange("a e d -> e a d")).then_inc(s_in, 16)
            sp.dma_start(maski, dr["mask"].rearrange("b s -> (b s)").partition_broadcast(P)).then_inc(s_in, 16)
            with nc.allow_non_contiguous_dma(reason="one mask value a descriptor, 2048 of them once"):
                sp.dma_start(qmaski, dr["mask"].rearrange("b (t p) -> p (b t)", p=P)).then_inc(s_in, 16)
            sp.dma_start(st["maskf"][:], dr["causal"]).then_inc(s_in, 16)

        @block.tensor
        def _(pe):
            pe.wait_ge(s_ctx, 32)
            for c in range(NC):
                for k in range(4):
                    t = 4 * c + k
                    ins = pe.transpose(ps[:, c, k * P:(k + 1) * P], ao[:, t * D:(t + 1) * D], ident[:])
                ins.then_inc(s_t, 1)

        @block.gpsimd
        def _(pool):
            pool.memset(st["Ks"][:], 1.0)
            pool.memset(st["V"][:], 1.0)

        @block.scalar
        def _(act):
            for c in range(NC):
                act.wait_ge(s_t, c + 1)
                act.copy(ctxT[:, c * CH:(c + 1) * CH], ps[:, c, :])
            act.wait_ge(s_in, 128)
            act.activation(st["gate"][:], rows[:, R_OFF["g"]:R_OFF["g"] + 8], ACT.Tanh)

        @block.vector
        def _(dve):
            dve.memset(st["minus"][:], -1.0)
            dve.memset(st["neghalf"][:], -0.5)
            dve.memset(st["Qs"][:], 1.0)
            dve.wait_ge(s_ctx, 32)
            dve.tensor_copy(st["identb"][:], ident[:])
            dve.tensor_copy(st["identh"][:], ident[:])
            dve.wait_ge(s_in, 128)
            dve.tensor_copy(st["maskb"][:], st["maskf"][:])
            dve.tensor_copy(st["b2h"][:, 0], b2[:])
            dve.drain()
            dve.tensor_tensor(st["b2h"][:, 1], b2[:], st["b2h"][:, 0], ALU.subtract)
            dve.tensor_scalar(st["keep"][:], maski, 0.0, None, ALU.not_equal)
            dve.tensor_scalar(st["qkeep"][:], qmaski, 0.0, None, ALU.not_equal)
            for a in range(5):
                dve.tensor_scalar(st["qb"][:, a:a + 1], cols[:, C_OFF["q", a]:C_OFF["q", a] + 1],
                                  float(ATT[a]["dk"]) ** -0.5, None, ALU.mult)


def norm_statistics(nc, st, dve, s_var):
    x, stats, mom = st["x"], st["stats"], st["mom"]
    for t in range(NT):
        dve.bn_stats(stats[:, t, :], x[:, t * D:(t + 1) * D])
    dve.drain()
    dve.tensor_tensor(mom[:, 0, :], stats[:, :, 1], stats[:, :, 4], ALU.add)
    dve.tensor_tensor(mom[:, 1, :], stats[:, :, 1], stats[:, :, 4], ALU.subtract)
    dve.tensor_tensor(mom[:, 2, :], stats[:, :, 2], stats[:, :, 5], ALU.add)
    dve.drain()
    dve.tensor_tensor(mom[:, 3, :], mom[:, 1, :], mom[:, 1, :], ALU.mult)
    dve.tensor_scalar(mom[:, 4, :], mom[:, 0, :], 0.5, None, ALU.mult)
    dve.tensor_scalar(mom[:, 2, :], mom[:, 2, :], 1.0 / D, EPS, ALU.mult, ALU.add)
    dve.drain()
    dve.scalar_tensor_tensor(mom[:, 5, :], mom[:, 3, :], 0.25, mom[:, 2, :], ALU.mult, ALU.add).then_inc(s_var, 1)


def norm_vector(nc, st, dve, s_rstd, s_xn):
    dve.drain()
    dve.wait_ge(s_rstd, 1)
    for t in range(NT):
        tile = slice(t * D, (t + 1) * D)
        ins = dve.tensor_scalar(st["xn"][:, tile], st["x"][:, tile], st["mom"][:, 4, t:t + 1],
                                st["rstd"][:, t:t + 1], ALU.subtract, ALU.mult)
        if t % 4 == 3:
            ins.then_inc(s_xn, 1)


def norm_pool(nc, st, pool, s_var, s_rstd):
    pool.wait_ge(s_var, 1)
    pool.tensor_tensor(st["rstd"][:], st["mom"][:, 5, :], st["neghalf"][:], ALU.pow).then_inc(s_rstd, 1)


def norm_tensor(nc, st, pe, s_xn, s_xt, bank0):
    for c in range(NC):
        pe.wait_ge(s_xn, c + 1)
        for k in range(4):
            t = 4 * c + k
            ins = pe.transpose(st["ps"][:, bank0 + c, k * P:(k + 1) * P], st["xn"][:, t * D:(t + 1) * D],
                               st["ident"][:])
        ins.then_inc(s_xt, 1)


def norm_scalar(nc, st, act, s_xt, s_xc, bank0):
    for c in range(NC):
        act.wait_ge(s_xt, c + 1)
        act.copy(st["xnT"][:, c * CH:(c + 1) * CH], st["ps"][:, bank0 + c, :]).then_inc(s_xc, 1)


def norm_stage(nc, st, sem, tag):
    ended = sem.next_stage()
    s_var, s_rstd, s_xn, s_xt, s_xc = (sem(f"{tag}_{k}") for k in ("var", "rstd", "xn", "xt", "xc"))
    with nc.Block() as block:
        @block.vector
        def _(dve):
            norm_statistics(nc, st, dve, s_var)
            norm_vector(nc, st, dve, s_rstd, s_xn)

        @block.gpsimd
        def _(pool):
            pool.sem_clear(ended)
            norm_pool(nc, st, pool, s_var, s_rstd)

        @block.tensor
        def _(pe):
            norm_tensor(nc, st, pe, s_xn, s_xt, 4)

        @block.scalar
        def _(act):
            norm_scalar(nc, st, act, s_xt, s_xc, 4)


def project_stage(nc, st, sem, a, dr):
    ended = sem.next_stage()
    own = a == 4
    ps, wp, cols, rows, V, vf = (st[k] for k in ("ps", "wp", "cols", "rows", "V", "vf"))
    kf, rem, parts, biasrow = (st[k] for k in ("kf", "rem", "parts", "biasrow"))
    src = st["xnT"] if own else st["ctxT"]
    att = ATT[a]
    masked = att["keymask"]
    s_var, s_rstd, s_xn, s_xt, s_xc = (sem(f"p{a}_{k}") for k in ("var", "rstd", "xn", "xt", "xc"))
    projected = sem(f"p{a}_projected")
    evacuated = [sem(f"p{a}_evacuated_{k}") for k in "kq"]
    first = sem(f"p{a}_first_part")
    less_first = sem(f"p{a}_less_first")
    second = sem(f"p{a}_second_part")
    third = sem(f"p{a}_third_part")
    written = [sem(f"p{a}_written{k}") for k in range(4)]
    v_projected, v_copied, v_first, v_less_first, v_second, v_split = (
        sem(f"p{a}_{k}") for k in ("v_projected", "v_copied", "v_first", "v_less_first", "v_second", "v_split"))
    bias_made, bias_written, first_loaded = (sem(f"p{a}_{k}") for k in ("bias_made", "bias_written", "first_loaded"))
    IT = 2 * NC

    def w(k):
        o = W_OFF[k, a]
        return wp[:, o:o + D]

    def values_parts(c):
        return (vf[:, c % 2, :].rearrange("p (t h d) -> p t h d", t=4, h=H),
                [V[:, 4 * c:4 * c + 4, :, i * DH:(i + 1) * DH] for i in range(3)])

    def wait_evacuated(eng, i):
        eng.wait_ge(evacuated[i // NC], i % NC + 1)

    with nc.Block() as block:
        @block.tensor
        def _(pe):
            def project(i):
                if i >= 2:
                    wait_evacuated(pe, i - 2)
                data, c = (src, i) if i < NC else (st["xnT"], i - NC)
                if i >= NC and not own:
                    pe.wait_ge(s_xc, c + 1)
                pe.matmul(ps[:, i % 2, :], w("kq"[i // NC]), data[:, c * CH:(c + 1) * CH],
                          start=True, stop=True).then_inc(projected, 1)

            def values(c):
                if c >= 2:
                    pe.wait_ge(v_copied, c - 1)
                for k in range(4):
                    t = 4 * c + k
                    ins = pe.matmul(ps[:, 2 + c % 2, k * P:(k + 1) * P], src[:, t * P:(t + 1) * P], w("v"),
                                    start=True, stop=True)
                ins.then_inc(v_projected, 1)

            project(0)
            project(1)
            values(0)
            values(1)
            project(2)
            values(2)
            if not own:
                norm_tensor(nc, st, pe, s_xn, s_xt, 4)
            project(3)
            values(3)
            for i in range(NC, IT):
                project(i)

        @block.scalar
        def _(act):
            def evacuate(i):
                which = "kq"[i // NC]
                act.wait_ge(projected, i + 1)
                if i >= 2:
                    act.wait_ge(less_first, i - 1)
                bias = st["qb"][:, a:a + 1] if which == "q" else cols[:, C_OFF["k", a]:C_OFF["k", a] + 1]
                act.activation(kf[:, i % 2, :], ps[:, i % 2, :], ACT.Identity, bias=bias,
                               scale=float(att["dk"]) ** -0.5 if which == "q" else 1.0).then_inc(
                                   evacuated[i // NC], 1)

            def split_values(c):
                if c < NC:
                    v, part = values_parts(c)
                    act.wait_ge(v_copied, c + 1)
                    act.copy(part[0], v).then_inc(v_first, 1)
                if c > 0:
                    v, part = values_parts(c - 1)
                    act.wait_ge(v_less_first, c)
                    act.copy(part[1], v).then_inc(v_second, 1)

            for i in range(IT + 1):
                if i < IT:
                    if i >= NC or not masked:
                        evacuate(i)
                    wait_evacuated(act, i)
                    if i >= 4:
                        act.wait_ge(written[i % 4], 48)
                    act.copy(parts[:, i % 4, 0, :], kf[:, i % 2, :]).then_inc(first, 1)
                if i >= 1:
                    act.wait_ge(less_first, i)
                    act.copy(parts[:, (i - 1) % 4, 1, :], rem[:, (i - 1) % 4, :]).then_inc(second, 1)
                if i == 1 and not own:
                    norm_scalar(nc, st, act, s_xt, s_xc, 4)
                if 2 <= i <= NC + 2:
                    split_values(i - 2)
                if i == IT:
                    act.wait_ge(written[0], 96)
                    act.wait_ge(bias_written, 16)
                    for u in range(2):
                        load_unit(st, act, u, 0, u, first_loaded)
        @block.gpsimd
        def _(pool):
            pool.sem_clear(ended)
            if not own:
                norm_pool(nc, st, pool, s_var, s_rstd)
            for c in range(NC):
                v, part = values_parts(c)
                pool.wait_ge(v_first, c + 1)
                pool.tensor_tensor(v, v, part[0], ALU.subtract).then_inc(v_less_first, 1)
                pool.wait_ge(v_second, c + 1)
                pool.tensor_tensor(part[2], v, part[1], ALU.subtract).then_inc(v_split, 1)

        @block.vector
        def _(dve):
            def evacuate_masked(i):
                dve.wait_ge(projected, i + 1)
                if i >= 2:
                    dve.wait_ge(less_first, i - 1)
                dve.scalar_tensor_tensor(kf[:, i % 2, :], ps[:, i % 2, :], cols[:, C_OFF["k", a]:C_OFF["k", a] + 1],
                                         st["keep"][:, i * CH:(i + 1) * CH], ALU.add,
                                         ALU.mult).then_inc(evacuated[0], 1)

            def take_first(i):
                dve.wait_ge(first, i + 1)
                if i >= 4:
                    dve.wait_ge(third, i - 3)
                dve.tensor_tensor(rem[:, i % 4, :], kf[:, i % 2, :], parts[:, i % 4, 0, :],
                                  ALU.subtract).then_inc(less_first, 1)

            def third_part(i):
                dve.wait_ge(second, i + 1)
                dve.tensor_tensor(parts[:, i % 4, 2, :], rem[:, i % 4, :], parts[:, i % 4, 1, :],
                                  ALU.subtract).then_inc(third, 1)

            def add_value_bias(c):
                dve.wait_ge(v_projected, c + 1)
                if c >= 2:
                    dve.wait_ge(v_split, c - 1)
                dve.tensor_tensor(
                    vf[:, c % 2, :].rearrange("p (t d) -> p t d", t=4),
                    ps[:, 2 + c % 2, :].rearrange("p (t d) -> p t d", t=4),
                    bc(rows[:, R_OFF["v", a]:R_OFF["v", a] + D].rearrange("p (o d) -> p o d", o=1), [P, 4, D]),
                    ALU.add).then_inc(v_copied, 1)

            if not own:
                norm_statistics(nc, st, dve, s_var)
            if masked:
                cm = cols[0:48, C_OFF["cmask", a]:C_OFF["cmask", a] + 1]
                dve.tensor_scalar(biasrow, st["keep"][0:48, :], 1.0, cm, ALU.subtract,
                                  ALU.mult).then_inc(bias_made, 1)
                evacuate_masked(0)
                evacuate_masked(1)
            else:
                dve.memset(biasrow, 0.0).then_inc(bias_made, 1)
            add_value_bias(0)
            take_first(0)
            if not own:
                norm_vector(nc, st, dve, s_rstd, s_xn)
            for i in range(IT + 1):
                if 0 < i < IT:
                    take_first(i)
                if masked and i + 2 < NC and i < IT:
                    evacuate_masked(i + 2)
                if i >= 1:
                    third_part(i - 1)
                if 0 < i < NC:
                    add_value_bias(i)

        @block.sync
        def _(sp):
            if a == 0:
                sp.dma_start(st["sel"][:], dr["sel"]).then_inc(st["wsem"][0], 16)
            elif a < 4:
                load_experts(nc, st, sp, a, dr)
            sp.wait_ge(bias_made, 1)
            sp.dma_start(st["scrK"][RT:RB].rearrange("a h t -> (a h) t"), biasrow).then_inc(bias_written, 16)
            for i in range(IT):
                scr, order = ((st["scrK"], K_PARTS), (st["scrQ"], Q_PARTS))[i // NC]
                rows_of = scr[0:RT].rearrange("(g d) h t -> (d h) g t", d=DH)
                sp.wait_ge(third, i + 1)
                for part in range(3):
                    g = [j for j, q in enumerate(order) if q == part]
                    step = g[1] - g[0] if len(g) > 1 else 1
                    dst = rows_of[:, g[0]:g[-1] + 1:step, i % NC * CH:(i % NC + 1) * CH]
                    data = parts[:, i % 4, part, :].rearrange("p (o t) -> p o t", o=1)
                    sp.dma_start(dst, bc(data, [P, len(g), CH])).then_inc(written[i % 4], 16)
            for k in range(4):
                sp.wait_ge(written[k], 96)
            sp.wait_ge(bias_written, 16)
            sp.wait_ge(first_loaded, 2 * 32)


def load_unit(st, queue, slot, batch, half, loaded):
    for dst, src, n in ((st["Qs"], st["scrQ"], RT), (st["Ks"], st["scrK"], RB)):
        queue.dma_start(dst[0:n, slot, :, :],
                        src[:, half * HU:half * HU + HU, bass.ds(batch, S)]).then_inc(loaded, 16)


def load_experts(nc, st, sp, l, dr):
    for i, k in enumerate(("wg", "wu", "wd") if l == 1 else ("w1", "w2")):
        n = MOE[l]["cols"]
        sp.dma_start(st["wf"][:, i * n:(i + 1) * n], dr[f"L{l}_{k}"]).then_inc(st["wsem"][l], 16)


def attend_stage(nc, st, sem, a, dr):
    ended = sem.next_stage()
    att = ATT[a]
    causal = att["causal"]
    ps, Qs, Ks, prob, probhi, problo, V, ao = (
        st[k] for k in ("ps", "Qs", "Ks", "prob", "probhi", "problo", "V", "ao"))
    identb, maskb = st["identb"], st["maskb"]
    bmax, nmax, nparts, nmT, rsum, osum = (st[k] for k in ("bmax", "nmax", "nparts", "nmT", "rsum", "osum"))
    scrQ, scrK, scrM = st["scrQ"], st["scrK"], st["scrM"]
    NB = 3 if causal else 2
    BW = 128 if causal else 256
    W1 = 384 if causal else 512
    m0, m1 = {None: (None, None), "incl": (0, 0), "strict": (2, 1)}[causal]
    loaded = [sem(f"a{a}_loaded{k}") for k in range(4)]
    rows_done = sem(f"a{a}_rows_done")
    rows_read = sem(f"a{a}_rows_read")
    heads_read = sem(f"a{a}_heads_read")
    scored = sem(f"a{a}_scored")
    exped = sem(f"a{a}_exped")
    rest0 = sem(f"a{a}_rest0")
    rest1 = sem(f"a{a}_rest1")
    weighted = sem(f"a{a}_weighted")
    normed = sem(f"a{a}_normed")
    divided = sem(f"a{a}_divided")
    maxparts = sem(f"a{a}_maxparts")
    maxout = sem(f"a{a}_max_out")
    passed = sem(f"a{a}_passed")
    maxin = sem(f"a{a}_max_in")
    w_first = sem(f"a{a}_w_first")
    w_second = sem(f"a{a}_w_second")
    wf, whi = st["wf"], st["whi"]
    wparts = wf[:].bitcast(F16).rearrange("p (c two) -> p two c", two=2)
    cut = MOE[a]["mats"] * MOE[a]["cols"] // NU if a < 4 else 0

    def lin(it, k, per_unit, base):
        v = per_unit * k + base
        return v + 4 * per_unit * it if isinstance(it, int) else it * (4 * per_unit) + v

    def slots(eng, group, finish, filled=lambda: None, ahead=1):
        def slot(it, k):
            for g in range(ahead, 4):
                group(it, k, g)
            if not isinstance(it, int) or k < 3:
                for g in range(ahead):
                    group(it, k + 1, g)
            finish(it, k)
        for g in range(ahead):
            group(0, 0, g)
        filled()
        with eng.Fori(0, NU // 4 - 1) as it:
            for k in range(4):
                slot(it, k)
        for k in range(4):
            slot(NU // 4 - 1, k)

    def nothing(it, k):
        pass

    def heads_left(it, k):
        return not isinstance(it, int) or 4 * it + k < NU - 2

    def maxima_left(it, k):
        return not isinstance(it, int) or 4 * it + k < NU - 1

    def maxima_item(it, k):
        return 2 if heads_left(it, k) else 0

    def bank_of(k, j):
        return 4 + (k + 1 + j) % 2

    def weights_at(it, k):
        return slice(cut * (4 * it + k), cut * (4 * it + k + 1)) if isinstance(it, int) else \
            bass.ds(it * (4 * cut) + k * cut, cut)

    def rest(eng, it, k, g, i):
        eng.wait_ge(weighted, lin(it, k, 4, g + 1))
        eng.wait_ge(exped, lin(it, k, 4, g + 3))
        eng.tensor_tensor(problo[:, g % 2, i, 0:W1], prob[:, g % 2, i, 0:W1], probhi[:, g % 2, i, 0:W1],
                          ALU.subtract).then_inc((rest0, rest1)[i], 1)

    with nc.Block() as block:
        @block.gpsimd
        def _(pool):
            pool.sem_clear(ended)
            pool.sem_inc(divided, 2)

            def split_maxima(par, unit_plus_1):
                pool.wait_ge(heads_read, unit_plus_1)
                b = bmax[:, par]
                pool.tensor_tensor(nmax[:, 0, :, :].rearrange("p q h -> p h q"), b[:, :, 0:2],
                                   bc(st["minus"][:], [P, HU, 2]), ALU.mult)
                pool.drain()
                pool.tensor_copy(nparts[:, :, 0, :], nmax[:, 0, :, :])
                pool.drain()
                pool.tensor_tensor(nmax[:, 1, :, :], nmax[:, 0, :, :], nparts[:, :, 0, :], ALU.subtract)
                pool.drain()
                pool.tensor_copy(nparts[:, :, 1, :], nmax[:, 1, :, :])
                pool.drain()
                pool.tensor_tensor(nparts[:, :, 2, :], nmax[:, 1, :, :], nparts[:, :, 1, :],
                                   ALU.subtract).then_inc(maxparts, 1)

            def group(it, k, g):
                rest(pool, it, k, g, 1)
                if cut and g == 1:
                    w = weights_at(it, k)
                    pool.wait_ge(w_first, lin(it, k, 1, 1))
                    pool.tensor_tensor(wparts[:, 1, w], wf[:, w], whi[:, (k % 2) * cut:(k % 2 + 1) * cut],
                                       ALU.subtract).then_inc(w_second, 1)
                if g == 3 and heads_left(it, k):
                    split_maxima(k % 2, lin(it, k, 1, 3))

            def finish(it, k):
                pool.wait_ge(normed, lin(it, k, 1, 3))
                dst = ao[:, bass.ds(it * (4 * D) + (k // 2) * 2 * D, 2 * D)].rearrange("p (q x) -> p q x", q=2)
                dst = dst[:, :, 64 * (k % 2):64 * (k % 2) + 64].rearrange("p q (h d) -> p q h d", h=HU)
                pool.tensor_tensor(dst, osum[:, k % 2].rearrange("p (q h) d -> p q h d", q=2),
                                   bc(rsum[:, k % 2].rearrange("p (q h o) -> p q h o", q=2, o=1),
                                      [P, 2, HU, DH]), ALU.mult).then_inc(divided, 1)
            split_maxima(0, 1)
            split_maxima(1, 2)
            slots(pool, group, finish, ahead=2)

        @block.tensor
        def _(pe):
            pe.sem_inc(weighted, 2)

            def keep_warm(n, bank=0, col=0):
                for _ in range(n):
                    pe.matmul(ps[:, bank, col:], identb[:], st["keep"][:, col:CH], start=True, stop=True)

            def head_rows(slot, h, bank, item):
                pe.wait_ge(rows_read, item + 1)
                M = ps[:, bank, :]
                q, kk = Qs[0:RB, slot, h, :], Ks[0:RB, slot, h, :]
                if causal:
                    pe.matmul(M[:, 0:128], q[:, 0:128], kk[:, 0:128], start=True, stop=False)
                    pe.matmul(M[:, 0:128], identb[:], maskb[:, m0, :], start=False, stop=True)
                    pe.matmul(M[:, 128:256], q[:, 128:256], kk[:, 0:128], start=True, stop=True)
                    pe.matmul(M[:, 256:384], q[:, 128:256], kk[:, 128:256], start=True, stop=False)
                    ins = pe.matmul(M[:, 256:384], identb[:], maskb[:, m1, :], start=False, stop=True)
                else:
                    pe.matmul(M[:, 0:256], q[:, 0:128], kk[:, 0:256], start=True, stop=True)
                    ins = pe.matmul(M[:, 256:512], q[:, 128:256], kk[:, 0:256], start=True, stop=True)
                ins.then_inc(rows_done, 1)

            def max_rows(bank, item, unit_plus_1):
                pe.wait_ge(rows_read, item + 1)
                pe.wait_ge(maxparts, unit_plus_1)
                out = ps[:, bank, :].bitcast(BF16)
                for qt in range(2):
                    ins = pe.transpose(out[0:24, qt * 128:qt * 128 + 128],
                                       nparts[:, qt, :, :].rearrange("p a h -> p (a h)"), identb[:])
                ins.then_inc(rows_done, 1)

            def scores(it, k, g):
                pe.wait_ge(exped, lin(it, k, 4, g + 1))
                for i in range(2):
                    h = 2 * g + i
                    O = ps[:, 2 * (g % 2) + i, :]
                    q, kk = Qs[0:RM, k % 4, h, :], Ks[0:RM, k % 4, h, :]
                    if causal:
                        pe.matmul(O[:, 0:128], kk[:, 0:128], q[:, 0:128], start=True, stop=False)
                        pe.matmul(O[:, 0:128], maskb[:, m0, :], identb[:], start=False, stop=True)
                        pe.matmul(O[:, 128:256], kk[:, 0:128], q[:, 128:256], start=True, stop=True)
                        pe.matmul(O[:, 256:384], kk[:, 128:256], q[:, 128:256], start=True, stop=False)
                        ins = pe.matmul(O[:, 256:384], maskb[:, m1, :], identb[:], start=False, stop=True)
                    else:
                        pe.matmul(O[:, 0:256], kk[:, 0:128], q[:, 0:256], start=True, stop=True)
                        ins = pe.matmul(O[:, 256:512], kk[:, 128:256], q[:, 0:256], start=True, stop=True)
                ins.then_inc(scored, 1)

            def values(it, k, g):
                if g == 0:
                    pe.wait_ge(normed, lin(it, k, 1, 1))
                if causal:
                    keep_warm(3, 6 + k % 2, 2 * HU * VW)
                vf = V[:].rearrange("p t h w -> p (t h w)")
                for i in range(2):
                    h = 2 * g + i
                    pe.wait_ge((rest0, rest1)[i], lin(it, k, 4, g + 1))
                    for qt in range(2):
                        o = ps[:, 6 + k % 2, (qt * HU + h) * VW:(qt * HU + h + 1) * VW]
                        kts = [0] if causal and qt == 0 else [0, 1]
                        for kt in kts:
                            off = qt * 128 if kt == 0 else 256 + (0 if causal else qt * 128)
                            at = ((2 * (k // 2) + kt) * H + HU * (k % 2) + h) * VW
                            v = vf[:, bass.ds(it * (4 * H * VW) + at, VW)]
                            pe.matmul(o, probhi[:, g % 2, i, off:off + 128], v, start=(kt == 0), stop=False)
                            ins = pe.matmul(o, problo[:, g % 2, i, off:off + 128], v, start=False,
                                            stop=(kt == kts[-1]))
                ins.then_inc(weighted, 1)

            def group(it, k, g):
                v = (k + 2) % 4
                if g == 0:
                    pe.wait_ge(maxin, lin(it, k, 16, 16))
                scores(it, k, g)
                if g == 1 and maxima_left(it, k):
                    j = maxima_item(it, k)
                    max_rows(bank_of(k, j), lin(it, k, 9, 17 + j), lin(it, k, 1, 2))
                if heads_left(it, k):
                    if g == 0:
                        pe.wait_ge(loaded[v], lin(it, 0, 8, 32 * ((k + 2) // 4 + 1)))
                    for h in (2 * g, 2 * g + 1):
                        j = h + (g > 0)
                        head_rows(v, h, bank_of(k, j), lin(it, k, 9, 17 + j))
                if g > 0:
                    values(it, k, g - 1)

            for h in range(HU):
                head_rows(0, h, 4 + h % 2, h)
            for h in range(HU):
                if h == HU // 2:
                    max_rows(4, 12, 1)
                item = 8 + h + (h >= HU // 2)
                head_rows(1, h, 4 + item % 2, item)
            keep_warm(WARM)
            slots(pe, group, lambda it, k: values(it, k, 3), lambda: keep_warm(WARM // 2, 7))

        @block.scalar
        def _(act):
            act.sem_inc(exped, 2)

            def group(it, k, g):
                act.wait_ge(weighted, lin(it, k, 4, g + 1))
                act.wait_ge(scored, lin(it, k, 4, g + 1))
                act.activation(prob[:, g % 2, :, 0:W1], ps[:, 2 * (g % 2):2 * (g % 2) + 2, 0:W1],
                               ACT.Exp).then_inc(exped, 1)
                first = whi[:, (k % 2) * cut:(k % 2 + 1) * cut]
                if cut and g == 0:
                    act.copy(first, wf[:, weights_at(it, k)]).then_inc(w_first, 1)
                if cut and g == 3:
                    act.wait_ge(w_second, lin(it, k, 1, 1))
                    act.copy(wparts[:, 0, weights_at(it, k)], first)
            if cut:
                act.wait_ge(st["wsem"][a], 16 * MOE[a]["mats"])
            slots(act, group, nothing)

        @block.vector
        def _(dve):
            dve.sem_inc(rows_read, 2)
            dve.sem_inc(normed, 2)

            def read_head(par, h, bank, item):
                dve.wait_ge(rows_done, item + 1)
                ins = dve.tensor_reduce(bmax[:, par, h, 0:NB],
                                        ps[:, bank, 0:NB * BW].rearrange("p (n w) -> p n w", n=NB), AX.X, ALU.max)
                ins.then_inc(rows_read, 1)
                if h == HU - 1:
                    dve.drain()
                    b = bmax[:, par]
                    if causal:
                        dve.tensor_tensor(b[:, :, 1], b[:, :, 1], b[:, :, 2], ALU.max).then_inc(heads_read, 1)
                    else:
                        dve.sem_inc(heads_read, 1)

            def read_max_rows(par, bank, item, written):
                dve.wait_ge(maxout, written)
                dve.wait_ge(rows_done, item + 1)
                dve.tensor_copy(nmT[:, par, :], ps[0:24, bank, :].bitcast(BF16)[:, 0:S]).then_inc(rows_read, 1)

            def group(it, k, g):
                if g == 1 and maxima_left(it, k):
                    j = maxima_item(it, k)
                    read_max_rows((k + 1) % 2, bank_of(k, j), lin(it, k, 9, 17 + j), lin(it, k, 16, 32))
                if heads_left(it, k):
                    for h in (2 * g, 2 * g + 1):
                        j = h + (g > 0)
                        read_head(k % 2, h, bank_of(k, j), lin(it, k, 9, 17 + j))
                rest(dve, it, k, g, 0)

            def finish(it, k):
                dve.wait_ge(divided, lin(it, k, 1, 1))
                dve.wait_ge(weighted, lin(it, k, 4, 6))
                o = ps[:, 6 + k % 2, 0:2 * HU * VW].rearrange("p (n w) -> p n w", w=VW)
                dve.reciprocal(rsum[:, k % 2], o[:, :, 3 * DH])
                dve.tensor_reduce(osum[:, k % 2], o[:, :, 0:3 * DH].rearrange("p n (a d) -> p n d a", a=3), AX.X,
                                  ALU.add).then_inc(normed, 1)

            for h in range(HU):
                read_head(0, h, 4 + h % 2, h)
            for h in range(HU):
                if h == HU // 2:
                    read_max_rows(0, 4, 12, 16)
                item = 8 + h + (h >= HU // 2)
                read_head(1, h, 4 + item % 2, item)
            slots(dve, group, finish, ahead=2)

        @block.sync
        def _(sp):
            sp.sem_inc(maxout, 32)

            def maxima(par, slot, item, before, after):
                wait_apart(sp, rows_read, item + 3, passed)
                sp.wait_ge(maxin, before)
                sp.dma_start(scrM[par], nmT[:, par, :]).then_inc(maxout, 16)
                sp.wait_ge(maxout, after)
                sp.dma_start(Qs[RB:RM, slot, :, :],
                             scrM[par].rearrange("(a h) q -> a h q", a=3)).then_inc(maxin, 16)

            for u in range(2):
                sp.sem_inc(loaded[u], 32)
                load_unit(st, sp, 2 + u, S, u, loaded[2 + u])
            sp.wait_ge(rows_read, 12 + 3)
            sp.dma_start(scrM[0], nmT[:, 0, :]).then_inc(maxout, 16)
            sp.wait_ge(maxout, 48)
            sp.dma_start(Qs[RB:RM, 0, :, :], scrM[0].rearrange("(a h) q -> a h q", a=3)).then_inc(maxin, 16)

            def slot(it, k):
                if maxima_left(it, k):
                    item = lin(it, k, 9, 17 + maxima_item(it, k))
                    before, after = lin(it, k, 16, 16), lin(it, k, 16, 64)
                    maxima((k + 1) % 2, (k + 1) % 4, item, before, after)
                if not isinstance(it, int):
                    at = sp.snap(it * (2 * S) + (k // 2 + 2) * S)
                    wait_apart(sp, scored, lin(it, k, 4, 4), passed)
                    load_unit(st, sp, k, at, k % 2, loaded[k])
            with sp.Fori(0, NU // 4 - 1) as it:
                for k in range(4):
                    slot(it, k)
            for k in range(4):
                slot(NU // 4 - 1, k)


def output_stage(nc, st, sem, a):
    ended = sem.next_stage()
    own = a == 4
    ps, x, xnT, ao, kf, rows, cols = (st[k] for k in ("ps", "x", "xnT", "ao", "kf", "rows", "cols"))
    wo = st["wp"][:, W_OFF["o", a]:W_OFF["o", a] + D]
    s_t, s_c, s_o = (sem(f"o{a}_{k}") for k in ("transposed", "copied", "projected"))
    with nc.Block() as block:
        @block.gpsimd
        def _(pool):
            pool.sem_clear(ended)

        @block.tensor
        def _(pe):
            def turn(c):
                for k in range(4):
                    t = 4 * c + k
                    ins = pe.transpose(ps[:, c, k * P:(k + 1) * P], ao[:, t * D:(t + 1) * D], st["ident"][:])
                ins.then_inc(s_t, 1)
            turn(0)
            for c in range(NC):
                if c + 1 < NC:
                    turn(c + 1)
                pe.wait_ge(s_c, c + 1)
                if own:
                    ins = pe.matmul(ps[:, 4 + c, :], wo, kf[:, c % 2, :], start=True, stop=True)
                else:
                    for k in range(4):
                        ins = pe.matmul(ps[:, 4 + c, k * P:(k + 1) * P], kf[:, c % 2, k * P:(k + 1) * P], wo,
                                        start=True, stop=True)
                ins.then_inc(s_o, 1)

        @block.scalar
        def _(act):
            for c in range(NC):
                act.wait_ge(s_t, c + 1)
                if c >= 2:
                    act.wait_ge(s_o, c - 1)
                act.copy(kf[:, c % 2, :], ps[:, c, :]).then_inc(s_c, 1)
                if own and c >= 1:
                    act.wait_ge(s_o, c)
                    act.activation(xnT[:, (c - 1) * CH:c * CH], ps[:, 4 + c - 1, :], ACT.Identity,
                                   bias=cols[:, C_OFF["o", 4]:C_OFF["o", 4] + 1])
            if own:
                act.wait_ge(s_o, NC)
                act.activation(xnT[:, 3 * CH:], ps[:, 7, :], ACT.Identity,
                               bias=cols[:, C_OFF["o", 4]:C_OFF["o", 4] + 1])

        if not own:
            @block.vector
            def _(dve):
                bo = rows[:, R_OFF["o", a]:R_OFF["o", a] + D]
                for c in range(NC):
                    dve.wait_ge(s_o, c + 1)
                    xc = x[:, c * CH:(c + 1) * CH]
                    if a == 0:
                        for k in range(4):
                            t = 4 * c + k
                            dve.scalar_tensor_tensor(ao[:, t * D:(t + 1) * D], ps[:, 4 + c, k * P:(k + 1) * P],
                                                     st["qkeep"][:, t:t + 1], bo, ALU.mult, ALU.add)
                    else:
                        dve.tensor_tensor(ao[:, c * CH:(c + 1) * CH].rearrange("p (t d) -> p t d", t=4),
                                          ps[:, 4 + c, :].rearrange("p (t d) -> p t d", t=4),
                                          bc(bo.rearrange("p (o d) -> p o d", o=1), [P, 4, D]), ALU.add)
                    dve.drain()
                    dve.scalar_tensor_tensor(xc, ao[:, c * CH:(c + 1) * CH], st["gate"][:, a:a + 1], xc,
                                             ALU.mult, ALU.add)


def route_stage(nc, st, sem, l, dr):
    ended = sem.next_stage()
    ps, xnT, wp, rows, rt, top, small, coef = (
        st[k] for k in ("ps", "xnT", "wp", "rows", "rt", "top", "small", "coef"))
    E = MOE[l]["E"]
    own = l == 3
    s_var, s_rstd, s_xn, s_xt, s_xc = (sem(f"r{l}_{k}") for k in ("var", "rstd", "xn", "xt", "xc"))
    s_l, s_d, s_a, s_c, s_t = (sem(f"r{l}_{k}") for k in ("logits", "shifted", "exps", "coefs", "turned"))
    lg = ps[:, 0:2, :].rearrange("p b c -> p (b c)")[:, 0:NT * E].rearrange("p (t e) -> p t e", e=E)
    A, Bf, Cf, Df = (rt[:, i, :, 0:E] for i in range(4))

    xh = st["xh"]
    s_xh = sem(f"r{l}_x_first")

    def wide(v, e=E):
        return bc(v.rearrange("p (t o) -> p t o", o=1), [P, NT, e])

    with nc.Block() as block:
        @block.tensor
        def _(pe):
            if not own:
                norm_tensor(nc, st, pe, s_xn, s_xt, 4)
            for t in range(NT):
                if not own and t % 4 == 0:
                    pe.wait_ge(s_xc, t // 4 + 1)
                ins = pe.matmul(lg[:, t, :], xnT[:, t * P:(t + 1) * P], wp[:, W_OFF["r", l]:W_OFF["r", l] + E],
                                start=True, stop=True)
            ins.then_inc(s_l, 1)
            pe.wait_ge(s_c, 1)
            turned = ps[:, 2:4, :].rearrange("p b c -> p (b c)").bitcast(F16)
            for t in range(NT):
                ins = pe.transpose(turned[0:2 * E, t * P:(t + 1) * P], coef[:, t, 0:2 * E], st["identh"][:])
            ins.then_inc(s_t, 1)

        @block.gpsimd
        def _(pool):
            pool.sem_clear(ended)
            if not own:
                norm_pool(nc, st, pool, s_var, s_rstd)
            if l > 0:
                for c in range(NC):
                    pool.wait_ge(s_xh, c + 1)
                    sl = slice(c * CH, (c + 1) * CH)
                    pool.tensor_tensor(xh[:, 1, sl], xnT[:, sl], xh[:, 0, sl], ALU.subtract)

        @block.scalar
        def _(act):
            if not own:
                norm_scalar(nc, st, act, s_xt, s_xc, 4)
            if l > 0:
                for c in range(NC):
                    if not own:
                        act.wait_ge(s_xc, c + 1)
                    act.copy(xh[:, 0, c * CH:(c + 1) * CH], xnT[:, c * CH:(c + 1) * CH]).then_inc(s_xh, 1)
            if l == 1:
                act.wait_ge(s_l, 1)
                act.activation(A, lg, ACT.Sigmoid).then_inc(s_a, 1)
            else:
                act.wait_ge(s_d, 1)
                act.activation(Bf, Bf, ACT.Exp).then_inc(s_a, 1)
            act.wait_ge(s_t, 1)
            turned = ps[:, 2:4, :].rearrange("p b c -> p (b c)").bitcast(F16)
            act.copy(st["coefT"][0:2 * E, :], turned[0:2 * E, :])

        @block.vector
        def _(dve):
            if not own:
                norm_statistics(nc, st, dve, s_var)
                norm_vector(nc, st, dve, s_rstd, s_xn)
            dve.wait_ge(s_l, 1)
            if l == 1:
                G = 8
                eb = bc(rows[:, R_OFF["ebias"]:R_OFF["ebias"] + E].rearrange("p (o e) -> p o e", o=1), [P, NT, E])
                dve.wait_ge(s_a, 1)
                dve.tensor_tensor(Bf, A, eb, ALU.add)
                dve.drain()
                g4 = [v.rearrange("p t (g e) -> p (t g) e", g=G) for v in (A, Bf, Cf, Df)]
                m1, m2, cnt, gs = (small[:, i, :, :] for i in range(4))
                m1f, m2f, cntf = (v.rearrange("p t (g o) -> p (t g) o", o=1) for v in (m1, m2, cnt))
                dve.tensor_reduce(m1f, g4[1], AX.X, ALU.max)
                dve.drain()
                dve.tensor_tensor(g4[2], g4[1], bc(m1f, [P, NT * G, 8]), ALU.is_equal)
                dve.drain()
                dve.tensor_reduce(cntf, g4[2], AX.X, ALU.add)
                dve.scalar_tensor_tensor(Df.rearrange("p t e -> p (t e)"), Cf.rearrange("p t e -> p (t e)"), -BIG,
                                         Bf.rearrange("p t e -> p (t e)"), ALU.mult, ALU.add)
                dve.drain()
                dve.tensor_reduce(m2f, g4[3], AX.X, ALU.max)
                dve.tensor_scalar(cnt, cnt, 1.5, None, ALU.is_ge)
                dve.drain()
                dve.tensor_tensor(gs, cnt, m1, ALU.mult)
                dve.tensor_scalar(cnt, cnt, 1.0, BIG, ALU.subtract, ALU.mult)
                dve.drain()
                dve.tensor_tensor(gs, gs, cnt, ALU.add)
                dve.drain()
                dve.tensor_tensor(gs, gs, m2, ALU.max)
                dve.drain()
                dve.tensor_tensor(gs, gs, m1, ALU.add)
                dve.drain()
                for t in range(NT):
                    dve.max(top[:, t, :], gs[:, t, :])
                dve.drain()
                dve.tensor_tensor(gs, gs, wide(top[:, :, 3], G), ALU.is_ge)
                dve.drain()
                dve.tensor_tensor(g4[2], g4[1], bc(gs.rearrange("p t (g o) -> p (t g) o", o=1), [P, NT * G, 8]),
                                  ALU.mult)
                dve.drain()
                for t in range(NT):
                    dve.max(top[:, t, :], Cf[:, t, :])
                dve.drain()
                for t in range(NT):
                    dve.match_replace(Df[:, t, :], top[:, t, :], Cf[:, t, :], -BIG)
                dve.drain()
                dve.tensor_scalar(Df, Df, -BIG / 2, None, ALU.is_le)
                dve.drain()
                dve.tensor_tensor(Bf, A, Df, ALU.mult)
                scale, tiny = 2.5, 1e-20
            else:
                if l == 2:
                    dve.tensor_copy(A, lg)
                else:
                    rb = rows[:, R_OFF["r", l]:R_OFF["r", l] + E].rearrange("p (o e) -> p o e", o=1)
                    dve.tensor_tensor(A, lg, bc(rb, [P, NT, E]), ALU.add)
                dve.drain()
                for t in range(NT):
                    dve.max(top[:, t, :], A[:, t, :])
                dve.drain()
                dve.tensor_tensor(Bf, A, wide(top[:, :, 0]), ALU.subtract).then_inc(s_d, 1)
                dve.tensor_tensor(Cf, A, wide(top[:, :, 0 if l == 2 else 1]), ALU.is_ge)
                dve.drain()
                dve.wait_ge(s_a, 1)
                scale, tiny = {0: (2.0, None), 2: (1.0, None), 3: (0.3, 1e-8)}[l]
                s0 = small[:, 0, :, 0]
                if l != 0:
                    dve.tensor_reduce(s0, Bf, AX.X, ALU.add)
                    dve.drain()
                    dve.reciprocal(s0, s0)
                    dve.drain()
                    dve.tensor_tensor(Bf, Bf, wide(s0), ALU.mult)
                    dve.drain()
                dve.tensor_tensor(Bf, Bf, Cf, ALU.mult)
            dve.drain()
            if l != 2:
                s1 = small[:, 1, :, 0]
                dve.tensor_reduce(s1, Bf, AX.X, ALU.add)
                dve.drain()
                if tiny:
                    dve.tensor_scalar(s1, s1, tiny, None, ALU.add)
                    dve.drain()
                dve.reciprocal(s1, s1)
                dve.drain()
                dve.tensor_scalar(s1, s1, scale, None, ALU.mult)
                dve.drain()
                dve.tensor_tensor(Bf, Bf, wide(s1), ALU.mult)
                dve.drain()
            dve.tensor_copy(coef[:, :, 0:E], Bf)
            dve.drain()
            dve.tensor_tensor(coef[:, :, E:2 * E], Bf, coef[:, :, 0:E], ALU.subtract).then_inc(s_c, 1)



def adapter_stage(nc, st, sem):
    ended = sem.next_stage()
    ps, x, xnT, wp, hid, sel, coefT = (st[k] for k in ("ps", "x", "xnT", "wp", "hid", "sel", "coefT"))
    E = MOE[0]["E"]
    up, acted, weighed, down = (sem(f"e0_{k}") for k in ("up", "copied", "weighed", "down"))
    GB, CB, YB = 0, 2, 4
    g = st["gate"][:, 4:5]
    base, down_w, up_w = (wp[:, W_OFF[k]:W_OFF[k] + D] for k in ("base", "loraB", "loraA"))
    with nc.Block() as block:
        @block.gpsimd
        def _(pool):
            pool.sem_clear(ended)

        @block.tensor
        def _(pe):
            def do_up(c):
                chunk = slice(c * CH, (c + 1) * CH)
                if c == 0:
                    pe.wait_ge(st["wsem"][0], 16)
                if c >= 2:
                    pe.wait_ge(weighed, c - 1)
                pe.matmul(ps[:, GB + c % 2, :], up_w, xnT[:, chunk], start=True, stop=True)
                pe.matmul(ps[:, CB + c % 2, :], sel[0:2 * E, SEL_OFF[0]:SEL_OFF[0] + P], coefT[0:2 * E, chunk],
                          start=True, stop=True).then_inc(up, 1)

            do_up(0)
            for c in range(NC):
                if c + 1 < NC:
                    do_up(c + 1)
                for k in range(4):
                    tok = slice(c * CH + k * P, c * CH + (k + 1) * P)
                    y = ps[:, YB + c, k * P:(k + 1) * P]
                    pe.matmul(y, xnT[:, tok], base, start=True, stop=False)
                    if k == 0:
                        pe.wait_ge(weighed, c + 1)
                    ins = pe.matmul(y, hid[:, c % 2, 1, k * P:(k + 1) * P], down_w, start=False, stop=True)
                ins.then_inc(down, 1)

        @block.scalar
        def _(act):
            for c in range(NC):
                if c >= 2:
                    act.wait_ge(weighed, c - 1)
                act.wait_ge(up, c + 1)
                act.copy(hid[:, c % 2, 0, :], ps[:, GB + c % 2, :]).then_inc(acted, 1)

        @block.vector
        def _(dve):
            x3 = x[:].rearrange("p (t d) -> p t d", d=D)
            bias = st["rows"][:, R_OFF["base"]:R_OFF["base"] + D].rearrange("p (o d) -> p o d", o=1)
            dve.scalar_tensor_tensor(x3, bc(bias, [P, NT, D]), g, x3, ALU.mult, ALU.add)
            for c in range(NC):
                dve.wait_ge(acted, c + 1)
                if c >= 2:
                    dve.wait_ge(down, c - 1)
                dve.tensor_tensor(hid[:, c % 2, 1, :], hid[:, c % 2, 0, :], ps[:, CB + c % 2, :],
                                  ALU.mult).then_inc(weighed, 1)
            for c in range(NC):
                dve.wait_ge(down, c + 1)
                xc = x[:, c * CH:(c + 1) * CH]
                dve.scalar_tensor_tensor(xc, ps[:, YB + c, :], g, xc, ALU.mult, ALU.add)


def expert_stage(nc, st, sem, l):
    ended = sem.next_stage()
    ps, x, xn, xh, wf, cols, hid, hparts, yT, sel, coefT, b2h = (
        st[k] for k in ("ps", "x", "xn", "xh", "wf", "cols", "hid", "hparts", "yT", "sel", "coefT", "b2h"))
    m_ = MOE[l]
    E, f, N, per = m_["E"], m_["f"], m_["blocks"], 1 if l == 1 else 2
    gated = l == 1
    LAG = 3
    lead = LAG + 1 + (N - LAG - 1) % 4
    up, acted, weighed, first, second, down = (
        sem(f"e{l}_{k}") for k in ("up", "activated", "weighed", "first_part", "second_part", "down"))
    copied, turned, added = (sem(f"e{l}_{k}") for k in ("y_copied", "y_turned", "y_added"))
    GB, UB, CB, YB = 0, 2, 4, 6
    g = st["gate"][:, 4 + l:5 + l]
    wparts = wf[:].bitcast(F16).rearrange("p (c two) -> p two c", two=2)
    PRODUCTS = ((0, 0), (0, 1), (1, 0))

    def weight_parts(which, part, j):
        return wparts[:, part, bass.ds(j * P + which * N * P, P)]

    def steps(c, eng, body):
        for s in range(lead):
            body(s, s)
        with eng.Fori(0, (N - lead) // 4) as it:
            for k in range(4):
                body(it * 4 + (lead + k), lead + k)

    with nc.Block() as block:
        @block.gpsimd
        def _(pool):
            pool.sem_clear(ended)
            pool.sem_inc(second, 2)

            def split(c, s, r):
                m = N * c
                pool.wait_ge(first, s + (m + 1))
                pool.tensor_tensor(hparts[:, (m + r) % 4, 1, :], hid[:, (m + r) % 2, 1, :],
                                   hparts[:, (m + r) % 4, 0, :], ALU.subtract).then_inc(second, 1)
            for c in range(NC):
                steps(c, pool, lambda s, r: split(c, s, r))

        @block.tensor
        def _(pe):
            pe.sem_inc(down, 4)

            def product(out, which, j, c):
                for i, (wpart, xpart) in enumerate(PRODUCTS):
                    ins = pe.matmul(out, weight_parts(which, wpart, j), xh[:, xpart, c * CH:(c + 1) * CH],
                                    start=(i == 0), stop=(i == 2))
                return ins

            def do_up(c, s, r):
                m = N * c
                pe.wait_ge(weighed, s + (m + 1))
                if gated:
                    product(ps[:, UB + (m + r) % 2, :], 1, s, c)
                ins = product(ps[:, GB + (m + r) % 2, :], 0, s, c)
                if gated and isinstance(s, int) and s == 0:
                    pass
                elif gated:
                    ins = pe.matmul(ps[:, CB + (m + r) % 2, :],
                                    sel[0:2 * E, bass.ds(s * P + (SEL_OFF[l] - P), P)],
                                    coefT[0:2 * E, c * CH:(c + 1) * CH], start=True, stop=True)
                elif r % 2 == 0:
                    at = s * (P // 2) + SEL_OFF[l]
                    ins = pe.matmul(ps[:, CB + (m + r) // 2 % 2, :], sel[0:2 * E, bass.ds(at, P)],
                                    coefT[0:2 * E, c * CH:(c + 1) * CH], start=True, stop=True)
                ins.then_inc(up, 1)

            def do_down(c, s, r, opens, closes):
                m = N * c
                pe.wait_ge(second, s + (m + 3))
                for i, (wpart, hpart) in enumerate(PRODUCTS):
                    ins = pe.matmul(ps[:, YB + c % 2, :], weight_parts(m_["mats"] - 1, wpart, s),
                                    hparts[:, (m + r) % 4, hpart, :], start=(opens and i == 0),
                                    stop=(closes and i == 2))
                ins.then_inc(down, 1)

            def turn(c):
                pe.wait_ge(copied, c + 1)
                for k in range(4):
                    ins = pe.transpose(ps[:, YB + c % 2, k * P:(k + 1) * P], yT[:, k * P:(k + 1) * P],
                                       st["ident"][:])
                ins.then_inc(turned, 1)

            for c in range(NC):
                def step(s, r):
                    do_up(c, s, r)
                    if r < LAG:
                        if c > 0:
                            do_down(c - 1, N - LAG + r, N - LAG + r, False, r == LAG - 1)
                        return
                    if r == LAG:
                        if c >= 2:
                            pe.wait_ge(added, c - 1)
                        if l > 1:
                            for part in range(2):
                                pe.matmul(ps[:, YB + c % 2, :], b2h[0:2 * E, part, l - 2, :],
                                          coefT[0:2 * E, c * CH:(c + 1) * CH], start=(part == 0), stop=False)
                    do_down(c, s - LAG, r - LAG, r == LAG and l == 1, False)
                steps(c, pe, step)
                if c > 0:
                    turn(c - 1)
            for r in range(N - LAG, N):
                do_down(NC - 1, r, r, False, r == N - 1)
            turn(NC - 1)

        @block.scalar
        def _(act):
            def activate(c, s, r):
                m = N * c
                act.wait_ge(weighed, s + (m + 1))
                act.wait_ge(up, s + (m + 1))
                bias = 0.0 if l < 2 else cols[:, bass.ds(s + C_OFF["b1", l], 1)]
                act.activation(hid[:, (m + r) % 2, 0, :], ps[:, GB + (m + r) % 2, :], f,
                               bias=bias).then_inc(acted, 1)

            def first_part(c, s, r):
                m = N * c
                act.wait_ge(down, s + m)
                act.wait_ge(weighed, s + (m + 2))
                act.copy(hparts[:, (m + r - 1) % 4, 0, :], hid[:, (m + r - 1) % 2, 1, :]).then_inc(first, 1)

            def copy_output(c):
                if c > 0:
                    act.wait_ge(turned, c)
                act.wait_ge(down, N * (c + 1) + 4)
                act.copy(yT, ps[:, YB + c % 2, :]).then_inc(copied, 1)

            for c in range(NC):
                def step(s, r):
                    activate(c, s, r)
                    if c > 0 or r > 0:
                        first_part(c, s, r)
                    if c > 0 and r == LAG:
                        copy_output(c - 1)
                steps(c, act, step)
            first_part(NC, 0, 0)
            copy_output(NC - 1)

        @block.vector
        def _(dve):
            dve.sem_inc(weighed, 2)
            if l == 3:
                dve.scalar_tensor_tensor(x[:], xn[:], g, x[:], ALU.mult, ALU.add)

            def weigh(c, s, r):
                m = N * c
                h0, h1 = hid[:, (m + r) % 2, 0, :], hid[:, (m + r) % 2, 1, :]
                coef = ps[:, CB + (m + r) // per % 2, :]
                dve.wait_ge(acted, s + (m + 1))
                dve.wait_ge(second, s + (m + 1))
                if gated and isinstance(s, int) and s == 0:
                    dve.tensor_tensor(h1, h0, ps[:, UB + (m + r) % 2, :], ALU.mult).then_inc(weighed, 1)
                    return
                if gated:
                    dve.tensor_tensor(h0, h0, ps[:, UB + (m + r) % 2, :], ALU.mult)
                    dve.drain()
                dve.tensor_tensor(h1, h0, coef, ALU.mult).then_inc(weighed, 1)

            def add(c):
                dve.wait_ge(turned, c + 1)
                xc = x[:, c * CH:(c + 1) * CH]
                dve.scalar_tensor_tensor(xc, ps[:, YB + c % 2, :], g, xc, ALU.mult, ALU.add).then_inc(added, 1)

            for c in range(NC):
                steps(c, dve, lambda s, r: weigh(c, s, r))
                if c > 0:
                    add(c - 1)
            add(NC - 1)


_OUT = (B, S, D)


def kernel(**inputs):
    import numpy as np
    import concourse.bacc as bacc
    from concourse.bass_utils import run_bass_kernel_spmd

    a = {k: np.asarray(v) for k, v in inputs.items()}

    def dims_major(w):
        return w.reshape(w.shape[0], H, DH).transpose(0, 2, 1).reshape(w.shape[0], H * DH)

    def pad_heads(w):
        return np.concatenate([w.reshape(w.shape[0], H, 4), np.zeros((w.shape[0], H, 4), np.float32)],
                              axis=2).reshape(w.shape[0], H * DH)

    xa = [{k: a[f"L{l}_xattn_{n}"].T for k, n in zip("qkvo", ("Wq", "Wk", "Wv", "Wo"))} for l in (0, 1, 3)]
    xa.insert(2, {k: a[f"L2_xattn_w_{k}"].T for k in "qkvo"})
    xa.append({"q": a["L3_ffn_q_w"], "k": pad_heads(a["L3_ffn_k_w"]), "v": pad_heads(a["L3_ffn_v_w"]),
               "o": pad_heads(a["L3_ffn_o_w"][0:64].T).T})
    zero = np.zeros((1, D), np.float32)
    bias = [{k: a[f"L0_xattn_b{k}"][None] for k in "qkvo"},
            {"q": zero, "k": zero, "v": a["L1_xattn_bv"][None], "o": a["L1_xattn_bo"][None]},
            {k: zero for k in "qkvo"},
            {k: a[f"L3_xattn_b{k}"][None] for k in "qkvo"},
            {"q": a["L3_ffn_q_b"][None], "k": pad_heads(a["L3_ffn_k_b"][None]),
             "v": pad_heads(a["L3_ffn_v_b"][None]), "o": a["L3_ffn_o_b"][None]}]
    w = []
    for m in xa:
        w += [dims_major(m["q"]), dims_major(m["k"]), m["v"], m["o"]]
    w += [a["L0_ffn_base_w"].T, a["L0_ffn_lora_A"].transpose(1, 0, 2).reshape(D, P),
          a["L0_ffn_lora_B"].reshape(P, D)]
    w += [a["L0_ffn_router_w"].T, a["L1_ffn_router_w"].T, a["L2_ffn_router_w"], a["L3_ffn_router_w"]]
    cols = []
    for m in bias:
        cols += [dims_major(m["q"]), dims_major(m["k"])]
    cols += [a["L0_ffn_base_b"][None], a["L2_ffn_b1"].reshape(28, P), a["L3_ffn_b1"].reshape(16, P), zero]

    def constant_rows(parts):
        out = np.zeros((1, D), np.float32)
        for i, p in enumerate(parts):
            out[0, 16 * i:16 * i + 16] = p
        return out

    cols += [constant_rows([BIG]), constant_rows([998244352.0, 1753088.0, 2560.0]), a["L3_ffn_o_b"][None]]
    rows = []
    for m in bias:
        rows += [m["v"], m["o"]]
    rows += [a["L0_ffn_base_b"][None], a["L0_ffn_router_b"][None], a["L3_ffn_router_b"][None], a["L1_ffn_e_bias"][None],
             a["g_xattn"][None], a["g_ffn"][None]]
    sel = np.zeros((P, SEL_N), np.float16)
    for l in range(4):
        E = MOE[l]["E"]
        n = {0: 1, 1: 32, 2: 14, 3: 8}[l]
        for i in range(n):
            for j in range(P):
                e = {0: j // 16, 1: 2 * i + j // 64}.get(l, i)
                sel[[e, e + E], SEL_OFF[l] + i * P + j] = 1
    low = np.tril(np.ones((P, P), np.float32))
    strict = np.tril(np.ones((P, P), np.float32), -1)
    strict0 = strict.copy()
    strict0[0, 0] = 1
    causal = np.stack([np.where(m > 0, 0.0, -BIG).astype(np.float32) for m in (low, strict, strict0)], axis=1)

    def pairs_of(g, s):
        return np.concatenate([s, g.transpose(1, 0, 2).reshape(D, 64 * 64)], axis=1)

    def down(w2):
        return w2.transpose(1, 0, 2).reshape(P, -1)

    b2 = np.zeros((2, 28, D), np.float32)
    b2[0, 0:14] = b2[0, 14:28] = a["L2_ffn_b2"]
    b2[1, 0:8] = b2[1, 8:16] = a["L3_ffn_b2"]
    arrays = {
        "x": a["x"], "ctx": a["ctx_1024"], "mask": a["mask_BxS2_ik0"],
        "wpack": np.concatenate(w, axis=1), "cols": np.concatenate(cols, axis=0).T, "rows": np.concatenate(rows, axis=1)[0],
        "b2": b2, "ident": np.eye(P, dtype=np.float32), "causal": causal, "sel": sel,
        "L1_wg": pairs_of(a["L1_ffn_Wg"], a["L1_ffn_SWg"]), "L1_wu": pairs_of(a["L1_ffn_Wu"], a["L1_ffn_SWu"]),
        "L1_wd": np.concatenate([a["L1_ffn_SWd"], down(a["L1_ffn_Wd"].reshape(32, P, D))], axis=1),
        "L2_w1": a["L2_ffn_w1"].transpose(1, 0, 2).reshape(D, 14 * 256),
        "L2_w2": down(a["L2_ffn_w2"].reshape(28, P, D)),
        "L3_w1": a["L3_ffn_w1"].transpose(1, 0, 2).reshape(D, 8 * 256),
        "L3_w2": down(a["L3_ffn_w2"].reshape(16, P, D)),
    }
    arrays = {k: np.ascontiguousarray(v) for k, v in arrays.items()}
    nc = bacc.Bacc("TRN2", target_bir_lowering=False, num_devices=1)
    dr = {k: nc.dram_tensor(f"in_{k}", v.shape, mybir.dt.from_np(v.dtype), kind="ExternalInput").ap()
          for k, v in arrays.items()}
    out = nc.dram_tensor("out", _OUT, F32, kind="ExternalOutput").ap()
    build(nc, dr, out)
    r = run_bass_kernel_spmd(nc, [{f"in_{k}": v for k, v in arrays.items()}], core_ids=[0])
    return r.results[0]["out"]
```
